# Optimizing a Trainium2 kernel written in Bass

```python
import numpy as np
import jax
import jax.numpy as jnp

def _softmax(x, axis=-1):
    return jax.nn.softmax(x, axis=axis)

def _gelu(x):
    return jax.nn.gelu(x, approximate=True)

def _silu(x):
    return jax.nn.silu(x)

def _sigmoid(x):
    return jax.nn.sigmoid(x)

def _layernorm(x, axis=-1, eps=1e-05):
    m = jnp.mean(x, axis=axis, keepdims=True)
    v = jnp.var(x, axis=axis, keepdims=True)
    return (x - m) / jnp.sqrt(v + eps)

def _scatter_add(tgt, idx, src, axis=0):
    return tgt.at[idx].add(src)

def _segment_sum(src, seg, n):
    return jax.ops.segment_sum(src, seg, n)
kernel_name = 'mk_adaln_attn_ffn_d1_seqx_r4_e42df1'

def setup_inputs(seed: int=0):
    np.random.seed(seed)
    _w = jnp.asarray

    def _rec_inputs():
        import jax
        import jax.numpy as jnp
        _rk = jax.random.key(seed)
        x = -7.109e-05 + 0.9999 * jax.random.normal(jax.random.fold_in(_rk, 1), (32, 64, 1024), jnp.float32)
        _lenS = 64 - jax.random.randint(jax.random.fold_in(_rk, 7), (32,), 0, max(1, 64 // 4) + 1, jnp.int32)
        _lenS2 = 64 - jax.random.randint(jax.random.fold_in(_rk, 8), (32,), 0, max(1, 64 // 4) + 1, jnp.int32)
        itok_B_0_15 = jax.random.randint(jax.random.fold_in(_rk, 11), (32,), 0, 16, jnp.int32)
        itok_B_1_14 = jax.random.randint(jax.random.fold_in(_rk, 12), (32,), 1, 15, jnp.int32)
        return (x, itok_B_0_15, itok_B_1_14)
    x, itok_B_0_15, itok_B_1_14 = _rec_inputs()

    def _L0_cond_setup():
        import jax, jax.numpy as jnp
        import numpy as np
        B, C, T = (64, 64, 1024)
        S, D = (16, 64)
        key = jax.random.key(seed)
        k1, k2, k3 = jax.random.split(key, 3)
        x = jax.random.normal(k1, (B, C, T), dtype=jnp.float32)
        condition = jax.random.randint(k2, (B,), 0, S, dtype=jnp.int64)
        bound = float(np.sqrt(6.0 / C))
        weights = jax.random.uniform(k3, (S, C, D), dtype=jnp.float32, minval=-bound, maxval=bound)
        return {'x': x, 'condition': condition, 'weights': weights}
    _L0_cond_all = _L0_cond_setup()
    _L0_cond_in = {k: v for k, v in _L0_cond_all.items() if k in ('weights',)}
    del _L0_cond_all

    def _L0_attn_setup():
        import jax, jax.numpy as jnp
        import numpy as np
        EMBED = 1024
        HEADS = 16
        HEAD_DIM = EMBED // HEADS
        ROT = 64
        B, S = (1, 512)
        MASK_VAL = -1000000000.0

        def _rotate_every_two(x):
            r = jnp.stack((x[..., 1::2], x[..., ::2]), axis=-1)
            return r.reshape(x.shape)

        def _fixed_pos_embedding(seq_len, rot_dim):
            inv_freq = 1.0 / 10000.0 ** (jnp.arange(0, rot_dim, 2, dtype=jnp.float32) / rot_dim)
            t = jnp.arange(seq_len, dtype=jnp.float32)
            sinusoid = jnp.einsum('i,j->ij', t, inv_freq)
            return (jnp.sin(sinusoid), jnp.cos(sinusoid))

        def _apply_rotary(x, sin, cos):
            sin = jnp.repeat(sin[None, :, None, :], 2, axis=3)
            cos = jnp.repeat(cos[None, :, None, :], 2, axis=3)
            return x * cos + _rotate_every_two(x) * sin
        key = jax.random.key(seed)
        ks = jax.random.split(key, 5)
        sc = 0.02
        return {'hidden_states': jax.random.normal(ks[0], (B, S, EMBED), jnp.float32), 'Wq': jax.random.normal(ks[1], (EMBED, EMBED), jnp.float32) * sc, 'Wk': jax.random.normal(ks[2], (EMBED, EMBED), jnp.float32) * sc, 'Wv': jax.random.normal(ks[3], (EMBED, EMBED), jnp.float32) * sc, 'Wo': jax.random.normal(ks[4], (EMBED, EMBED), jnp.float32) * sc}
    _L0_attn_all = _L0_attn_setup()
    _L0_attn_in = {k: v for k, v in _L0_attn_all.items() if k in ('Wq', 'Wk', 'Wv', 'Wo')}
    del _L0_attn_all

    def _L0_cond2_setup():
        import jax, jax.numpy as jnp
        import numpy as np
        B, S, D_IN = (8, 512, 1024)
        A, D_OUT = (16, 1024)
        key = jax.random.key(seed)
        k1, k2, k3 = jax.random.split(key, 3)
        x = jax.random.normal(k1, (B, S, D_IN), dtype=jnp.float32)
        weight = jax.random.normal(k2, (A, D_OUT, D_IN), dtype=jnp.float32) * 0.02
        adapter_ids = jax.random.randint(k3, (B,), 0, A, dtype=jnp.int64)
        return {'x': x, 'weight': weight, 'adapter_ids': adapter_ids}
    _L0_cond2_all = _L0_cond2_setup()
    _L0_cond2_in = {k: v for k, v in _L0_cond2_all.items() if k in ('weight',)}
    del _L0_cond2_all

    def _L0_ffn_setup():
        import jax, jax.numpy as jnp
        import numpy as np
        B, S, D = (4, 512, 1024)
        NUM_EXPERTS, TOP_K = (3, 2)

        def _expert_outputs(h, w1, b1, w2, b2):
            pre = jnp.einsum('bsd,edf->ebsf', h, w1) + b1[:, None, None, :]
            act = jnp.stack([jnp.tanh(pre[0]), jax.nn.gelu(pre[1], approximate=False), jax.nn.silu(pre[2])])
            return jnp.einsum('ebsf,efd->ebsd', act, w2) + b2[:, None, None, :]
        key = jax.random.key(seed)
        ks = jax.random.split(key, 8)
        scale_in = 1.0 / np.sqrt(D)
        scale_gate = 1.0 / np.sqrt(D + 1)
        return {'h': jax.random.normal(ks[0], (B, S, D), dtype=jnp.float32), 'gate_w': jax.random.uniform(ks[1], (D + 1, NUM_EXPERTS), minval=-scale_gate, maxval=scale_gate, dtype=jnp.float32), 'gate_b': jnp.zeros((NUM_EXPERTS,), dtype=jnp.float32), 'w1': jax.random.uniform(ks[2], (NUM_EXPERTS, D, D), minval=-scale_in, maxval=scale_in, dtype=jnp.float32), 'b1': jnp.zeros((NUM_EXPERTS, D), dtype=jnp.float32), 'w2': jax.random.uniform(ks[3], (NUM_EXPERTS, D, D), minval=-scale_in, maxval=scale_in, dtype=jnp.float32), 'b2': jnp.zeros((NUM_EXPERTS, D), dtype=jnp.float32)}
    _L0_ffn_all = _L0_ffn_setup()
    _L0_ffn_in = {k: v for k, v in _L0_ffn_all.items() if k in ('gate_w', 'gate_b', 'w1', 'b1', 'w2', 'b2')}
    del _L0_ffn_all
    return {'x': x, 'itok_B_0_15': itok_B_0_15, 'itok_B_1_14': itok_B_1_14, 'L0_cond_weights': _L0_cond_in['weights'], 'L0_attn_Wq': _L0_attn_in['Wq'], 'L0_attn_Wk': _L0_attn_in['Wk'], 'L0_attn_Wv': _L0_attn_in['Wv'], 'L0_attn_Wo': _L0_attn_in['Wo'], 'L0_cond2_weight': _L0_cond2_in['weight'], 'L0_ffn_gate_w': _L0_ffn_in['gate_w'], 'L0_ffn_gate_b': _L0_ffn_in['gate_b'], 'L0_ffn_w1': _L0_ffn_in['w1'], 'L0_ffn_b1': _L0_ffn_in['b1'], 'L0_ffn_w2': _L0_ffn_in['w2'], 'L0_ffn_b2': _L0_ffn_in['b2']}

def reference(x, itok_B_0_15, itok_B_1_14, L0_cond_weights, L0_attn_Wq, L0_attn_Wk, L0_attn_Wv, L0_attn_Wo, L0_cond2_weight, L0_ffn_gate_w, L0_ffn_gate_b, L0_ffn_w1, L0_ffn_b1, L0_ffn_w2, L0_ffn_b2):
    import jax
    import jax.numpy as jnp

    def _L0_cond_ref(x, condition, weights):
        import jax, jax.numpy as jnp
        import numpy as np
        B, C, T = (64, 64, 1024)
        S, D = (16, 64)
        W = weights[condition]
        return jnp.einsum('bct,bcd->bdt', x, W)

    def _L0_attn_ref(hidden_states, Wq, Wk, Wv, Wo):
        import jax, jax.numpy as jnp
        import numpy as np
        EMBED = 1024
        HEADS = 16
        HEAD_DIM = EMBED // HEADS
        ROT = 64
        B, S = (1, 512)
        MASK_VAL = -1000000000.0

        def _rotate_every_two(x):
            r = jnp.stack((x[..., 1::2], x[..., ::2]), axis=-1)
            return r.reshape(x.shape)

        def _fixed_pos_embedding(seq_len, rot_dim):
            inv_freq = 1.0 / 10000.0 ** (jnp.arange(0, rot_dim, 2, dtype=jnp.float32) / rot_dim)
            t = jnp.arange(seq_len, dtype=jnp.float32)
            sinusoid = jnp.einsum('i,j->ij', t, inv_freq)
            return (jnp.sin(sinusoid), jnp.cos(sinusoid))

        def _apply_rotary(x, sin, cos):
            sin = jnp.repeat(sin[None, :, None, :], 2, axis=3)
            cos = jnp.repeat(cos[None, :, None, :], 2, axis=3)
            return x * cos + _rotate_every_two(x) * sin
        b, s, e = hidden_states.shape
        q = (hidden_states @ Wq).reshape(b, s, HEADS, HEAD_DIM)
        k = (hidden_states @ Wk).reshape(b, s, HEADS, HEAD_DIM)
        v = (hidden_states @ Wv).reshape(b, s, HEADS, HEAD_DIM)
        sin, cos = _fixed_pos_embedding(s, ROT)
        q = jnp.concatenate([_apply_rotary(q[..., :ROT], sin, cos), q[..., ROT:]], axis=-1)
        k = jnp.concatenate([_apply_rotary(k[..., :ROT], sin, cos), k[..., ROT:]], axis=-1)
        q = q.transpose(0, 2, 1, 3)
        k = k.transpose(0, 2, 1, 3)
        v = v.transpose(0, 2, 1, 3)
        logits = jnp.einsum('bhqd,bhkd->bhqk', q, k)
        causal = jnp.tril(jnp.ones((s, s), dtype=bool))[None, None]
        logits = jnp.where(causal, logits, MASK_VAL)
        logits = logits / jnp.sqrt(jnp.float32(HEAD_DIM))
        attn = jax.nn.softmax(logits, axis=-1)
        out = jnp.einsum('bhqk,bhkd->bhqd', attn, v)
        out = out.transpose(0, 2, 1, 3).reshape(b, s, e)
        return out @ Wo

    def _L0_cond2_ref(x, weight, adapter_ids):
        import jax, jax.numpy as jnp
        import numpy as np
        B, S, D_IN = (8, 512, 1024)
        A, D_OUT = (16, 1024)
        w = weight[adapter_ids]
        return jnp.einsum('bij,bkj->bik', x, w)

    def _L0_ffn_ref(h, gate_w, gate_b, w1, b1, w2, b2):
        import jax, jax.numpy as jnp
        import numpy as np
        B, S, D = (4, 512, 1024)
        NUM_EXPERTS, TOP_K = (3, 2)

        def _expert_outputs(h, w1, b1, w2, b2):
            pre = jnp.einsum('bsd,edf->ebsf', h, w1) + b1[:, None, None, :]
            act = jnp.stack([jnp.tanh(pre[0]), jax.nn.gelu(pre[1], approximate=False), jax.nn.silu(pre[2])])
            return jnp.einsum('ebsf,efd->ebsd', act, w2) + b2[:, None, None, :]
        b, s, d = h.shape
        vision_len = int(s * 0.3)
        text_strength = jnp.mean(jnp.abs(h[:, vision_len:, :]), axis=(1, 2), keepdims=True)
        vision_strength = jnp.mean(jnp.abs(h[:, :vision_len, :]), axis=(1, 2), keepdims=True)
        modality_ratio = text_strength / (vision_strength + 1e-08)
        modality_ratio = jnp.broadcast_to(modality_ratio, (b, s, 1))
        router_input = jnp.concatenate([h, modality_ratio], axis=-1)
        gate_logits = router_input @ gate_w + gate_b
        gate_scores = jax.nn.softmax(gate_logits, axis=-1)
        top_val, top_idx = jax.lax.top_k(gate_scores, TOP_K)
        top_val = top_val / (jnp.sum(top_val, axis=-1, keepdims=True) + 1e-08)
        expert_out = _expert_outputs(h, w1, b1, w2, b2)
        moe_out = jnp.zeros_like(h)
        batch_idx = jnp.arange(b)
        for i in range(TOP_K):
            j = top_idx[:, 0, i]
            out_i = expert_out[j, batch_idx]
            moe_out = moe_out + top_val[..., i:i + 1] * out_i
        return moe_out
    x = x + _L0_attn_ref(_L0_cond_ref(x, itok_B_0_15, L0_cond_weights), L0_attn_Wq, L0_attn_Wk, L0_attn_Wv, L0_attn_Wo)
    x = x + _L0_ffn_ref(_L0_cond2_ref(x, L0_cond2_weight, itok_B_1_14), L0_ffn_gate_w, L0_ffn_gate_b, L0_ffn_w1, L0_ffn_b1, L0_ffn_w2, L0_ffn_b2)
    return x

_drawn_inputs = setup_inputs


def setup_inputs(seed=0):
    import zlib

    import numpy as np

    out = dict(_drawn_inputs(seed))
    spreads = {'L0_ffn_gate_b': (0.0, 0.1), 'L0_ffn_b1': (0.0, 0.29), 'L0_ffn_b2': (0.0, 0.1)}
    factors = {}
    for name, (base, spread) in spreads.items():
        noise = np.random.default_rng([zlib.crc32(name.encode()), seed]).standard_normal(out[name].shape)
        drawn = base * np.exp(spread * noise) if base else spread * noise
        out[name] = jnp.asarray(drawn.astype(out[name].dtype))
    for name, factor in factors.items():
        out[name] = (out[name] * factor).astype(out[name].dtype)
    return out
```

```python
from contextlib import ExitStack

import numpy as np

import concourse.bass as bass
from concourse import mybir

F32 = mybir.dt.float32
F32R = mybir.dt.float32r
I32 = mybir.dt.int32
ALU = mybir.AluOpType
ACT = mybir.ActivationFunctionType
AX = mybir.AxisListType

P = 128
B, T, D = 32, 64, 1024
HEADS, DH = 16, 64
NE = 3
BT = 512
BB = BT // T
NBLK = B * T // BT
NC = D // P
NP = BT // P
RING = 4
VISION = int(T * 0.3)

G_O = NC
G_AD = G_O + NC // RING
G_FF = G_AD + BB * NC // RING
G_ALL = G_FF + NE * 2 * NC // RING
FILLS = (G_ALL, G_ALL, G_ALL, G_ALL - NC)
USES = (2 * NC + NC // 2 + NE * NC, NC + NC // 2 + NE * NC)

C_ID, C_SEL, C_MASK, C_ROT, C_TEXT, C_VIS, C_END = 0, 128, 256, 384, 448, 576, 704


def shape_constants():
    c = np.zeros((P, C_END), np.float32)
    tok = np.arange(P)
    same = tok[:, None] // T == tok[None, :] // T
    c[:, C_ID:C_ID + P] = np.eye(P)
    c[:, C_SEL:C_SEL + P] = same & (tok[:, None] % T == 0)
    c[:, C_MASK:C_MASK + P] = np.where(same & (tok[None, :] <= tok[:, None]), 0.0, -1e30)
    freq = 1.0 / 10000.0 ** (np.arange(0, DH, 2) / DH)
    angle = freq[:, None] * np.arange(T)[None, :]
    plus, minus = np.cos(angle) + np.sin(angle), np.cos(angle) - np.sin(angle)
    c[:, C_ROT:C_ROT + T] = np.concatenate([plus, minus, plus, minus])
    c[VISION:T, C_TEXT:C_TEXT + P] = 1.0 / ((T - VISION) * D)
    c[0:VISION, C_VIS:C_VIS + P] = 1.0 / (VISION * D)
    return c


def build(nc, x_pairs, x_cols, ids_mix, ids_adapter, mix_w, wq, wk, wv, wo, adapter_w, gate_w,
          gate_last, gate_b, w1, b1, w2, b2, consts, out):
    ctx = ExitStack()
    with ctx:
        def sb(name, shape, dt=F32):
            return ctx.enter_context(nc.sbuf_tensor(name, shape, dt))

        def sem(name):
            return ctx.enter_context(nc.semaphore(name))

        raw = sb("raw", [P, RING, D])
        w_hi_t = sb("w_hi_t", [P, RING, D], F32R)
        w_lo_t = sb("w_lo_t", [P, RING, D], F32R)
        qk_land = sb("qk_land", [P, 2, NC, 2, 2, 32])
        a_hi = sb("a_hi", [P, NC, BT], F32R)
        a_lo = sb("a_lo", [P, NC, BT], F32R)
        b_hi = sb("b_hi", [P, NC, BT], F32R)
        b_lo = sb("b_lo", [P, NC, BT], F32R)
        xT = sb("xT", [P, NC, BT])
        x_nat = sb("x_nat", [P, NP, D])
        mix = sb("mix", [P, NP, P])
        mix_hi = sb("mix_hi", [P, NP, P], F32R)
        mix_lo = sb("mix_lo", [P, NP, P], F32R)
        rot = sb("rot", [P, 2, BT])
        qk_hi_t = sb("qk_hi_t", [P, 2, BT], F32R)
        qk_lo_t = sb("qk_lo_t", [P, 2, BT], F32R)
        vT = sb("vT", [P, BT])
        v_hi_t = sb("v_hi_t", [P, NP, P], F32R)
        v_lo_t = sb("v_lo_t", [P, NP, P], F32R)
        probs = sb("probs", [P, 2, NP, P])
        pt_hi_t = sb("pt_hi_t", [P, 2, BT], F32R)
        pt_lo_t = sb("pt_lo_t", [P, 2, BT], F32R)
        row_max = sb("row_max", [P, 2 * NP])
        row_sum = sb("row_sum", [P, 2 * NP])
        row_inv = sb("row_inv", [P, 2 * NP])
        y_nat = x_nat[0:T, 0:2, :]
        junk = x_nat[0:T, 2, :]
        abs_sum_t = sb("abs_sum_t", [T, BB])
        act_t = rot
        scaled_t = probs[:, :, :, :].rearrange("p h n k -> p h (n k)")
        cst = sb("cst", [P, C_END])
        gw = sb("gw", [P, NC, 4])
        gw_hi = sb("gw_hi", [P, NC, 4], F32R)
        gw_lo = sb("gw_lo", [P, NC, 4], F32R)
        gw_last = sb("gw_last", [P, NE])
        gb = sb("gb", [P, NE])
        b1_t = sb("b1_t", [P, NE, NC])
        b2_t = sb("b2_t", [P, NE, NC])
        idm = sb("idm", [1, B], I32)
        ida = sb("ida", [1, B], I32)
        vis_eps = sb("vis_eps", [P, BB])
        vis_inv = sb("vis_inv", [P, BB])
        ratio = sb("ratio", [P, NP])
        r_last = sb("r_last", [P, NP, NE])
        r_bias = sb("r_bias", [P, NP, NE])
        logit = sb("logit", [P, NP, NE])
        l_max = sb("l_max", [P, NP])
        shifted = sb("shifted", [P, NP, NE])
        e_exp = sb("e_exp", [P, NP, NE])
        e_sum = sb("e_sum", [P, NP])
        e_inv = sb("e_inv", [P, NP])
        score = sb("score", [P, NP, NE])
        gt = sb("gt", [P, 3, NP])
        ngt = sb("ngt", [P, 3, NP])
        rank = sb("rank", [P, NE, NP])
        pick = sb("pick", [P, 2, NE, NP])
        top = sb("top", [P, 8, NP])
        topn = sb("topn", [P, 2, NP])
        part = sb("part", [P, 2, NE, NP])
        coef = sb("coef", [P, NE, NP])
        coef_w = sb("coef_w", [P, NE, NP, P])

        banks = ctx.enter_context(nc.psum_tensor("banks", [P, 8, 512], F32))
        GB = [0, 1]
        SB = [2, 3]
        TB = [4, 5]
        RB = [6, 7]

        ident = cst[:, C_ID:C_ID + P]

        const_landed = sem("const_landed")
        mix_zeroed = sem("mix_zeroed")
        gw_zeroed = sem("gw_zeroed")
        raw_ready = [sem(f"raw_ready{s}") for s in range(RING)]
        qk_landed = [sem("q_landed"), sem("k_landed")]
        x_landed = sem("x_landed")
        mix_landed = sem("mix_landed")
        xT_landed = sem("xT_landed")
        w_hi = sem("w_hi")
        w_lo = sem("w_lo")
        x_hi, x_lo = sem("x_hi"), sem("x_lo")
        mixw_hi, mixw_lo = sem("mixw_hi"), sem("mixw_lo")
        gwr_hi, gwr_lo = sem("gwr_hi"), sem("gwr_lo")
        mixed = sem("mixed")
        h_hi, h_lo = sem("h_hi"), sem("h_lo")
        gemm_done = sem("gemm_done")
        drained = [sem("drained0"), sem("drained1")]
        qk_hi, qk_lo = sem("qk_hi"), sem("qk_lo")
        vt_done, v_hi, v_lo = sem("vt_done"), sem("v_hi"), sem("v_lo")
        score_done = sem("score_done")
        sm_mask, sm_max, sm_shift = sem("sm_mask"), sem("sm_max"), sem("sm_shift")
        sm_exp, sm_sum, sm_inv, sm_probs = sem("sm_exp"), sem("sm_sum"), sem("sm_inv"), sem("sm_probs")
        pt_done, pt_hi, pt_lo = sem("pt_done"), sem("pt_hi"), sem("pt_lo")
        pv_done, o_hi, o_lo = sem("pv_done"), sem("o_hi"), sem("o_lo")
        x1_hi, x1_lo = sem("x1_hi"), sem("x1_lo")
        y_copied, abs_summed = sem("y_copied"), sem("abs_summed")
        yt_done, y_hi, y_lo = sem("yt_done"), sem("y_hi"), sem("y_lo")
        router_mm, router_exp, picked_mm = sem("router_mm"), sem("router_exp"), sem("picked_mm")
        r_step = sem("r_step")
        coef_ready, coef_spread = sem("coef_ready"), sem("coef_spread")
        act_scaled, act_hi, act_lo = sem("act_scaled"), sem("act_hi"), sem("act_lo")
        bias_added = sem("bias_added")
        out_stored = sem("out_stored")
        xT_free = sem("xT_free")

        block = ctx.enter_context(nc.Block())

        O_USE = (2 * NC, NC)
        COEF_BANKS = [SB[1], TB[0], TB[1]]
        N_CONST = 8
        R_SHIFT, R_PICK, R_STEPS = 9, 21, 33

        @block.sync
        def _(sp):
            sp.dma_start(idm[:, :], ids_mix).then_inc(const_landed, 16)
            sp.dma_start(ida[:, :], ids_adapter).then_inc(const_landed, 16)
            sp.dma_start(cst[:, :], consts).then_inc(const_landed, 16)
            sp.wait_ge(gw_zeroed, 1)
            sp.dma_start(gw[:, :, 0:NE], gate_w).then_inc(const_landed, 16)
            sp.dma_start(gw_last[:, :], gate_last.to_broadcast((P, NE))).then_inc(const_landed, 16)
            sp.dma_start(gb[:, :], gate_b.to_broadcast((P, NE))).then_inc(const_landed, 16)
            sp.dma_start(b1_t[:, :, :], b1).then_inc(const_landed, 16)
            sp.dma_start(b2_t[:, :, :], b2).then_inc(const_landed, 16)
            sp.wait_ge(const_landed, 16 * N_CONST)
            sp.wait_ge(mix_zeroed, 1)

            def fill(grp, s, src):
                sp.wait_ge(w_hi, RING * grp + s + 1)
                sp.wait_ge(w_lo, RING * grp + s + 1)
                sp.dma_start(raw[:, s, :], src).then_inc(raw_ready[s], 16)

            with sp.Fori(0, NBLK) as blk:
                sp.dma_start(x_nat[:, :, :], x_pairs[blk, :, :, :]).then_inc(x_landed, 16)
                for b in range(BB):
                    i = sp.value_load(idm[0:1, bass.ds(blk * BB + b, 1)], min_val=0, max_val=15)
                    h = b % 2
                    sp.dma_start(mix[h * T:h * T + T, b // 2, h * T:h * T + T], mix_w[i, :, :])\
                      .then_inc(mix_landed, 16)
                with sp.Fori(0, NC) as m:
                    for j, w in enumerate((wq, wk)):
                        sp.wait_ge(w_hi, (blk * G_ALL + m) * RING + (j + 1))
                        sp.dma_start(qk_land[:, j], w[m, :, :]).then_inc(qk_landed[j], 16)
                    fill(blk * G_ALL + m, 2, wv[m, :, :])
                sp.wait_ge(xT_free, blk + 1)
                sp.dma_start(xT[:, :, :], x_cols[blk, :, :, :]).then_inc(xT_landed, 16)
                with sp.Fori(0, NC // RING) as g:
                    for s in range(RING):
                        fill(blk * G_ALL + G_O + g, s, wo[g * RING + s, :, :])
                with sp.Fori(0, BB) as b:
                    i = sp.value_load(ida[0:1, bass.ds(blk * BB + b, 1)], min_val=0, max_val=15)
                    for c in range(NC):
                        fill(blk * G_ALL + G_AD + b * 2 + c // RING, c % RING, adapter_w[i * NC + c, :, :])
                with sp.Fori(0, NE) as e:
                    for k, w in enumerate((w1, w2)):
                        for m in range(NC):
                            fill(blk * G_ALL + G_FF + e * 4 + k * 2 + m // RING, m % RING,
                                 w[e * NC + m, :, :])

        @block.gpsimd
        def _(pool):
            pool.memset(gw[:, :, :], 0.0).then_inc(gw_zeroed, 1)
            pool.memset(mix[:, :, :], 0.0).then_inc(mix_zeroed, 1)
            pool.sem_inc(xT_free, 1)
            with pool.Fori(0, NBLK) as blk:
                with pool.Fori(0, NC) as m:
                    slab = pool.snap(blk * NC + m)
                    grp = pool.snap(blk * G_ALL + m)
                    for j in range(2):
                        r = raw[:, j, :].rearrange("p (c h u i) -> p c h u i", c=NC, h=2, u=2)
                        pool.wait_ge(qk_landed[j], slab * 16 + 16)
                        pool.wait_ge(w_hi, grp * RING + (j + 1))
                        pool.wait_ge(w_lo, grp * RING + (j + 1))
                        even, odd = qk_land[:, j, :, :, 0, :], qk_land[:, j, :, :, 1, :]
                        pool.tensor_tensor(r[:, :, :, 0, :], even, odd, ALU.add)
                        pool.tensor_tensor(r[:, :, :, 1, :], even, odd, ALU.subtract)\
                            .then_inc(raw_ready[j], 16)
                for n in range(NC):
                    done = pool.snap(blk * USES[n % 2] + (USES[n % 2] - NC // 2 + n // 2 + 2))
                    pool.wait_ge(drained[n % 2], done)
                    pool.dma_start(out[blk, :, n, :], xT[:, n, :]).then_inc(out_stored, 16)
                pool.wait_ge(out_stored, blk * (16 * NC) + 16 * NC)
                pool.sem_inc(xT_free, 1)
            pool.wait_ge(out_stored, 16 * NC * NBLK)

        @block.tensor
        def _(pe):
            def three(dst, l_hi, l_lo, r_hi, r_lo, start, stop):
                pe.matmul(dst, l_hi, r_hi, start=start, stop=False)
                pe.matmul(dst, l_hi, r_lo, start=False, stop=False)
                return pe.matmul(dst, l_lo, r_hi, start=False, stop=stop)

            def wait_piece(grp, s):
                pe.wait_ge(w_hi, grp * RING + (s + 1 + RING))
                pe.wait_ge(w_lo, grp * RING + (s + 1 + RING))

            def chunks(s, bank, hi, lo, cs, chunk_ready=None):
                for c in cs:
                    if chunk_ready is not None:
                        ready_hi, ready_lo, base = chunk_ready
                        pe.wait_ge(ready_hi, base + (c + 1))
                        pe.wait_ge(ready_lo, base + (c + 1))
                    w = slice(c * P, c * P + P)
                    mm = three(banks[:, bank, :], w_hi_t[:, s, w], w_lo_t[:, s, w], hi[:, c, :],
                               lo[:, c, :], c == 0, c == NC - 1)
                return mm

            def gemm(grp, s, bank, use, hi, lo, chunk_ready=None):
                wait_piece(grp, s)
                pe.wait_ge(drained[bank], use + 1)
                return chunks(s, GB[bank], hi, lo, range(NC), chunk_ready)

            def turn_probs(slab):
                pe.wait_ge(sm_probs, slab + 1)
                for h in range(2):
                    for p in range(NP):
                        mm = pe.transpose(banks[:, TB[h], p * P:p * P + P], probs[:, h, p, :], ident)
                    mm.then_inc(pt_done, 1)

            def values(slab):
                pe.wait_ge(v_hi, slab + 1)
                pe.wait_ge(v_lo, slab + 1)
                for h in range(2):
                    pe.wait_ge(pt_hi, slab * 2 + (h + 1))
                    pe.wait_ge(pt_lo, slab * 2 + (h + 1))
                    for p in range(NP):
                        w = slice(p * P, p * P + P)
                        mm = three(banks[:, RB[h], w], v_hi_t[:, p, :], v_lo_t[:, p, :],
                                   pt_hi_t[:, h, w], pt_lo_t[:, h, w], True, True)
                mm.then_inc(pv_done, 1)

            def attention_slab(blk, m, first):
                grp = pe.snap(blk * G_ALL + m)
                slab = pe.snap(blk * NC + m)
                ready = (h_hi, h_lo, blk * NC) if first else None
                gemm(grp, 0, 0, blk * USES[0] + m * 2, a_hi, a_lo, ready).then_inc(gemm_done, 1)
                gemm(grp, 1, 1, blk * USES[1] + m, a_hi, a_lo).then_inc(gemm_done, 1)
                if not first:
                    turn_probs(slab - 1)
                gemm(grp, 2, 0, blk * USES[0] + m * 2 + 1, a_hi, a_lo).then_inc(gemm_done, 2)
                if not first:
                    values(slab - 1)
                pe.wait_ge(drained[0], blk * USES[0] + m * 2 + 3)
                for p in range(NP):
                    w = slice(p * P, p * P + P)
                    mm = pe.transpose(banks[:, TB[0], w], vT[:, w], ident)
                mm.then_inc(vt_done, 1)
                pe.wait_ge(qk_hi, slab * 2 + 2)
                pe.wait_ge(qk_lo, slab * 2 + 2)
                for p in range(NP):
                    for h in range(2):
                        w, r = slice(p * P, p * P + P), slice(h * DH, h * DH + DH)
                        mm = three(banks[:, SB[h], w], qk_hi_t[r, 0, w], qk_lo_t[r, 0, w],
                                   qk_hi_t[r, 1, w], qk_lo_t[r, 1, w], True, True)
                mm.then_inc(score_done, 1)

            def wait_y(blk, b):
                pe.wait_ge(y_copied, blk * BB + (b + 1))
                if b >= 2:
                    pe.wait_ge(y_hi, blk * BB + (b - 1))
                    pe.wait_ge(y_lo, blk * BB + (b - 1))

            def turn_y(b):
                for c in range(NC):
                    mm = pe.transpose(banks[:, RB[b % 2], c * T:c * T + T],
                                      y_nat[:, b % 2, c * P:c * P + P], cst[0:T, C_ID:C_ID + T])
                mm.then_inc(yt_done, 1)

            pe.wait_ge(const_landed, 16 * N_CONST)
            pe.wait_ge(gwr_hi, 1)
            pe.wait_ge(gwr_lo, 1)
            with pe.Fori(0, NBLK) as blk:
                pe.wait_ge(mixw_hi, blk + 1)
                pe.wait_ge(mixw_lo, blk + 1)
                pe.wait_ge(x_hi, blk * NP + NP)
                pe.wait_ge(x_lo, blk * NP + NP)
                xh = b_hi[:, :, :].rearrange("p (n a) t -> p n (a t)", n=NP)
                xl = b_lo[:, :, :].rearrange("p (n a) t -> p n (a t)", n=NP)
                mix_banks = SB + RB
                for c in range(NC):
                    if c >= 4:
                        pe.wait_ge(h_hi, blk * NC + (c - 3))
                        pe.wait_ge(h_lo, blk * NC + (c - 3))
                    for p in range(NP):
                        w = slice(c * P, c * P + P)
                        mm = three(banks[:, mix_banks[c % 4], p * P:p * P + P], xh[:, p, w], xl[:, p, w],
                                   mix_hi[:, p, :], mix_lo[:, p, :], True, True)
                    mm.then_inc(mixed, 1)

                attention_slab(blk, 0, True)
                with pe.Fori(1, NC) as m:
                    attention_slab(blk, m, False)

                last = pe.snap(blk * NC + (NC - 1))
                for n in range(2):
                    wait_piece(blk * G_ALL + G_O, n)
                    pe.wait_ge(drained[n], blk * USES[n] + (O_USE[n] + 1))
                    chunks(n, GB[n], b_hi, b_lo, range(NC - 1), (o_hi, o_lo, blk * NC) if n == 0 else None)
                turn_probs(last)
                values(last)
                for n in range(2):
                    chunks(n, GB[n], b_hi, b_lo, [NC - 1], (o_hi, o_lo, blk * NC)).then_inc(gemm_done, 1)
                for n in range(2, NC):
                    gemm(blk * G_ALL + (G_O + n // RING), n % RING, n % 2,
                         blk * USES[n % 2] + (O_USE[n % 2] + n // 2), b_hi, b_lo)\
                        .then_inc(gemm_done, 1)

                for b in range(BB):
                    y_banks = SB if b % 2 == 0 else TB
                    for c in range(NC):
                        s = c % RING
                        wait_piece(blk * G_ALL + (G_AD + 2 * b + c // RING), s)
                        if b == 0:
                            pe.wait_ge(x1_hi, blk * NC + (c + 1))
                            pe.wait_ge(x1_lo, blk * NC + (c + 1))
                        if c == 0 and b >= 2:
                            pe.wait_ge(y_copied, blk * BB + (b - 1))
                            pe.wait_ge(abs_summed, blk * BB + (b - 1))
                        if c == 2 and b >= 1:
                            wait_y(blk, b - 1)
                        t = slice(b * T, b * T + T)
                        for half in range(2):
                            w = slice(half * 512, half * 512 + 512)
                            mm = three(banks[0:T, y_banks[half], :], a_hi[:, c, t], a_lo[:, c, t],
                                       w_hi_t[:, s, w], w_lo_t[:, s, w], c == 0, c == NC - 1)
                        mm.then_inc(gemm_done, 1)
                        if c == 2 and b >= 1:
                            turn_y(b - 1)

                grp = pe.snap(blk * G_ALL + G_FF)
                wait_y(blk, BB - 1)
                pe.wait_ge(abs_summed, blk * BB + BB)
                pe.matmul(banks[:, SB[0], 0:BB], cst[0:T, C_TEXT:C_TEXT + P], abs_sum_t[:, :],
                          start=True, stop=True)
                pe.matmul(banks[:, SB[0], BB:2 * BB], cst[0:T, C_VIS:C_VIS + P], abs_sum_t[:, :],
                          start=True, stop=True)
                turn_y(BB - 1)
                pe.wait_ge(y_hi, blk * BB + BB)
                pe.wait_ge(y_lo, blk * BB + BB)
                for p in range(NP):
                    for c in range(NC):
                        w = slice(p * P, p * P + P)
                        mm = three(banks[:, SB[1], 4 * p:4 * p + 4], b_hi[:, c, w], b_lo[:, c, w],
                                   gw_hi[:, c, :], gw_lo[:, c, :], c == 0, c == NC - 1)
                mm.then_inc(router_mm, 1)

                def ffn_piece(e, k, g, s, chunk_ready=None):
                    n = e * 4 + k * 2 + g
                    hi, lo = ((b_hi, b_lo), (a_hi, a_lo))[k]
                    use = (O_USE[s % 2] + NC // 2)
                    gemm(blk * G_ALL + (n + G_FF), s, s % 2, blk * USES[s % 2] + (n * 2 + (use + s // 2)),
                         hi, lo, chunk_ready).then_inc(gemm_done, 1)

                def router_picks():
                    pe.wait_ge(r_step, blk * R_STEPS + R_PICK)
                    pe.matmul(banks[:, SB[0], 0:2 * NE * NP], cst[:, C_SEL:C_SEL + P],
                              pick[:, :, :, :].rearrange("p a e n -> p (a e n)"), start=True, stop=True)\
                        .then_inc(picked_mm, 1)

                def router_spread():
                    pe.wait_ge(coef_ready, blk + 1)
                    for e in range(NE):
                        for p in range(NP):
                            mm = pe.matmul(banks[:, COEF_BANKS[e], p * P:p * P + P], coef_w[:, e, p, :],
                                           ident, start=True, stop=True)
                    mm.then_inc(coef_spread, 1)

                for g in range(NC // RING):
                    for s in range(RING):
                        ffn_piece(0, 0, g, s)
                        if g == 0 and s == 0:
                            router_picks()
                        if g == 0 and s == 1:
                            router_spread()
                for e in range(NE):
                    if e > 0:
                        with pe.Fori(0, NC // RING) as g:
                            for s in range(RING):
                                ffn_piece(e, 0, g, s)
                    with pe.Fori(0, NC // RING) as g:
                        for s in range(RING):
                            ffn_piece(e, 1, g, s,
                                      (act_hi, act_lo, blk * (NE * NC) + e * NC) if s == 0 else None)


        @block.scalar
        def _(act):
            def copy(dst, src):
                return act.activation(dst, src, ACT.Copy)

            def split(fills, s, n=1):
                act.wait_ge(raw_ready[s], fills * 16 + 16)
                copy(w_hi_t[:, s, :], raw[:, s, :]).then_inc(w_hi, n)

            def fills(blk, grp, s):
                return blk * FILLS[s] + (grp - NC if s == 3 else grp)

            def attention_slab(blk, m, first):
                slab = act.snap(blk * NC + m)
                split(fills(blk, m, 2), 2, 2)
                if not first:
                    exp(slab - 1)
                act.wait_ge(drained[0], blk * USES[0] + m * 2 + 2)
                copy(qk_hi_t[:, 0, :], rot[:, 0, :]).then_inc(qk_hi, 1)
                split(fills(blk, m + 1, 0), 0)
                act.wait_ge(drained[1], blk * USES[1] + m + 2)
                copy(qk_hi_t[:, 1, :], rot[:, 1, :]).then_inc(qk_hi, 1)
                if not first:
                    probs_hi(slab - 1)
                split(fills(blk, m + 1, 1), 1)
                act.wait_ge(gemm_done, (blk * G_ALL + m) * RING + 4)
                copy(vT[:, :], banks[:, GB[0], :]).then_inc(drained[0], 1)
                if not first:
                    out_hi(slab - 1, m - 1)
                act.wait_ge(vt_done, slab + 1)
                copy(v_hi_t[:, :, :].rearrange("p n k -> p (n k)"), banks[:, TB[0], :]).then_inc(v_hi, 1)

            def exp(slab):
                act.wait_ge(sm_shift, slab + 1)
                pr = probs[:, :, :, :].rearrange("p h n k -> p (h n k)")
                act.activation(pr, pr, ACT.Exp).then_inc(sm_exp, 1)

            def probs_hi(slab):
                for h in range(2):
                    act.wait_ge(pt_done, slab * 2 + (h + 1))
                    copy(pt_hi_t[:, h, :], banks[:, TB[h], :]).then_inc(pt_hi, 1)

            def out_hi(slab, m):
                act.wait_ge(pv_done, slab + 1)
                copy(b_hi[0:DH, m, :], banks[0:DH, RB[0], :])
                copy(b_hi[DH:P, m, :], banks[DH:P, RB[1], :]).then_inc(o_hi, 1)

            act.sem_inc(w_hi, RING)
            act.wait_ge(const_landed, 16 * N_CONST)
            copy(gw_hi[:, :, :], gw[:, :, :]).then_inc(gwr_hi, 1)
            xh = b_hi[:, :, :].rearrange("p (n a) t -> p n (a t)", n=NP)
            with act.Fori(0, NBLK) as blk:
                act.wait_ge(mix_landed, blk * (16 * BB) + 16 * BB)
                copy(mix_hi[:, :, :], mix[:, :, :]).then_inc(mixw_hi, 1)
                act.wait_ge(x_landed, blk * 16 + 16)
                for p in range(NP):
                    copy(xh[:, p, :], x_nat[:, p, :]).then_inc(x_hi, 1)
                split(fills(blk, 0, 0), 0)
                split(fills(blk, 0, 1), 1)
                for c in range(NC):
                    act.wait_ge(mixed, blk * NC + (c + 1))
                    copy(a_hi[:, c, :], banks[:, (SB + RB)[c % 4], :]).then_inc(h_hi, 1)

                attention_slab(blk, 0, True)
                with act.Fori(1, NC) as m:
                    attention_slab(blk, m, False)
                last = act.snap(blk * NC + (NC - 1))
                exp(last)
                split(fills(blk, G_O, 2), 2)
                probs_hi(last)
                out_hi(last, NC - 1)

                def x1_piece(n):
                    act.wait_ge(drained[n % 2], blk * USES[n % 2] + (O_USE[n % 2] + n // 2 + 2))
                    copy(a_hi[:, n, :], xT[:, n, :]).then_inc(x1_hi, 1)

                for n in range(NC):
                    if n > 0:
                        split(fills(blk, G_O + (n + 2) // RING, (n + 2) % RING), (n + 2) % RING)
                    x1_piece(n)

                def y_out(b):
                    act.wait_ge(gemm_done, blk * (G_ALL * RING) + (G_AD + 2 * b + 2) * RING)
                    yb = (SB if b % 2 == 0 else TB)[0]
                    copy(y_nat[:, b % 2, :], banks[0:T, yb:yb + 2, :].rearrange("p a n -> p (a n)"))\
                        .then_inc(y_copied, 1)

                def y_magnitudes(b):
                    if b > 0:
                        act.wait_ge(abs_summed, blk * BB + b)
                    yb = (SB if b % 2 == 0 else TB)[0]
                    act.activation(junk, banks[0:T, yb:yb + 2, :].rearrange("p a n -> p (a n)"),
                                   ACT.Abs, accum_out=abs_sum_t[:, b:b + 1]).then_inc(abs_summed, 1)

                def y_turned(b):
                    act.wait_ge(yt_done, blk * BB + (b + 1))
                    copy(b_hi[:, :, b * T:b * T + T],
                         banks[:, RB[b % 2], :].rearrange("p (c t) -> p c t", c=NC)).then_inc(y_hi, 1)

                for b in range(BB):
                    for c in range(NC):
                        g = G_AD + 2 * b + (c + 2) // RING
                        act.wait_ge(gemm_done, (blk * G_ALL + (g - 1)) * RING + ((c + 2) % RING + 1))
                        split(fills(blk, g, (c + 2) % RING), (c + 2) % RING)
                        if c == 2 and b > 0:
                            y_magnitudes(b - 1)
                        if c == 4 and b > 0:
                            y_turned(b - 1)
                    y_out(b)
                y_magnitudes(BB - 1)
                y_turned(BB - 1)

                act.wait_ge(r_step, blk * R_STEPS + R_SHIFT)
                act.activation(e_exp[:, :, :], shifted[:, :, :], ACT.Exp).then_inc(router_exp, 1)

                def w1_piece(e, g, s, func):
                    n = e * 4 + g
                    split(fills(blk, G_FF + n + (1 if s >= 2 else 0), (s + 2) % RING), (s + 2) % RING)
                    act.wait_ge(gemm_done, (blk * G_ALL + (n + G_FF)) * RING + (s + 1))
                    act.activation(act_t[:, s % 2, :], banks[:, GB[s % 2], :], func,
                                   bias=b1_t[:, e, bass.ds(g * RING + s, 1)]).then_inc(drained[s % 2], 1)
                    act.wait_ge(act_scaled, blk * (NE * NC) + (g * RING + (e * NC + s + 1)))
                    copy(a_hi[:, g * RING + s, :], scaled_t[:, s % 2, :]).then_inc(act_hi, 1)

                def w2_piece(e, g, s, more=True):
                    n = e * 4 + 2 + g
                    act.wait_ge(gemm_done, (blk * G_ALL + (n + G_FF)) * RING + s)
                    if more:
                        split(fills(blk, G_FF + n + (1 if s >= 2 else 0), (s + 2) % RING), (s + 2) % RING)

                for e, func in enumerate((ACT.Tanh, ACT.Gelu, ACT.Silu)):
                    with act.Fori(0, NC // RING) as g:
                        for s in range(RING):
                            w1_piece(e, g, s, func)
                    if e < NE - 1:
                        with act.Fori(0, NC // RING) as g:
                            for s in range(RING):
                                w2_piece(e, g, s)
                    else:
                        for s in range(RING):
                            w2_piece(e, 0, s)
                        for s in range(RING):
                            w2_piece(e, 1, s, s < 2)
                act.wait_ge(gemm_done, (blk * G_ALL + G_ALL) * RING)

        @block.vector
        def _(dve):
            def minus(dst, src, hi):
                return dve.tensor_tensor(dst, src, hi.bitcast(F32), ALU.subtract)

            def lo_piece(blk, grp, s, n=1):
                dve.wait_ge(w_hi, (blk * G_ALL + grp) * RING + (s + 1 + RING))
                minus(w_lo_t[:, s, :], raw[:, s, :], w_hi_t[:, s, :]).then_inc(w_lo, n)

            rot_f = cst[:, C_ROT:C_ROT + T].rearrange("p (o t) -> p o t", o=1).to_broadcast((P, BB, T))
            mask = cst[:, C_MASK:C_MASK + P].rearrange("p (o t) -> p o t", o=1).to_broadcast((P, NP, P))

            def wide(t, k):
                return t.rearrange("p (n o) -> p n o", o=1).to_broadcast((P, t.shape[1], k))

            def rotate(blk, m, slab, j):
                dve.wait_ge(gemm_done, (blk * G_ALL + m) * RING + (j + 1))
                dve.tensor_tensor(rot[:, j, :].rearrange("p (b t) -> p b t", b=BB),
                                  banks[:, GB[j], :].rearrange("p (b t) -> p b t", b=BB), rot_f, ALU.mult)\
                    .then_inc(drained[j], 1)

            def rotated_lo(slab, j, rotated):
                dve.wait_ge(qk_hi, slab * 2 + (j + 1))
                dve.wait_ge(drained[j], rotated)
                minus(qk_lo_t[:, j, :], rot[:, j, :], qk_hi_t[:, j, :]).then_inc(qk_lo, 1)

            def softmax_shift(slab):
                dve.wait_ge(score_done, slab + 1)
                for h in range(2):
                    dve.scalar_tensor_tensor(
                        out=probs[:, h, :, :], in0=banks[:, SB[h], :].rearrange("p (n k) -> p n k", n=NP),
                        scalar=0.5 / DH ** 0.5, in1=mask, op0=ALU.mult, op1=ALU.add).then_inc(sm_mask, 1)
                pr = probs[:, :, :, :].rearrange("p h n k -> p (h n) k")
                dve.wait_ge(sm_mask, slab * 2 + 2)
                dve.tensor_reduce(row_max[:, :], pr, AX.X, ALU.max).then_inc(sm_max, 1)
                dve.wait_ge(sm_max, slab + 1)
                dve.tensor_tensor(pr, pr, wide(row_max[:, :], P), ALU.subtract).then_inc(sm_shift, 1)

            def softmax_scale(slab):
                pr = probs[:, :, :, :].rearrange("p h n k -> p (h n) k")
                dve.wait_ge(sm_exp, slab + 1)
                dve.tensor_reduce(row_sum[:, :], pr, AX.X, ALU.add).then_inc(sm_sum, 1)
                dve.wait_ge(sm_sum, slab + 1)
                dve.reciprocal(row_inv[:, :], row_sum[:, :]).then_inc(sm_inv, 1)
                dve.wait_ge(sm_inv, slab + 1)
                dve.tensor_tensor(pr, pr, wide(row_inv[:, :], P), ALU.mult).then_inc(sm_probs, 1)

            def probs_lo(slab):
                for h in range(2):
                    dve.wait_ge(pt_hi, slab * 2 + (h + 1))
                    minus(pt_lo_t[:, h, :], banks[:, TB[h], :], pt_hi_t[:, h, :]).then_inc(pt_lo, 1)

            def out_lo(slab, m):
                dve.wait_ge(o_hi, slab + 1)
                minus(b_lo[0:DH, m, :], banks[0:DH, RB[0], :], b_hi[0:DH, m, :])
                minus(b_lo[DH:P, m, :], banks[DH:P, RB[1], :], b_hi[DH:P, m, :]).then_inc(o_lo, 1)

            def attention_slab(blk, m, first):
                slab = dve.snap(blk * NC + m)
                lo_piece(blk, m, 2, 2)
                if not first:
                    softmax_scale(slab - 1)
                rotate(blk, m, slab, 0)
                lo_piece(blk, m + 1, 0)
                rotated_lo(slab, 0, blk * USES[0] + m * 2 + 2)
                rotate(blk, m, slab, 1)
                if not first:
                    probs_lo(slab - 1)
                lo_piece(blk, m + 1, 1)
                rotated_lo(slab, 1, blk * USES[1] + m + 2)
                if not first:
                    out_lo(slab - 1, m - 1)
                dve.wait_ge(v_hi, slab + 1)
                minus(v_lo_t[:, :, :].rearrange("p n k -> p (n k)"), banks[:, TB[0], :],
                      v_hi_t[:, :, :].rearrange("p n k -> p (n k)")).then_inc(v_lo, 1)
                softmax_shift(slab)

            def router_logits(blk):
                base = dve.snap(blk * R_STEPS)
                steps = [0]

                def step(ins):
                    ins.then_inc(r_step, 1)
                    steps[0] += 1
                    dve.wait_ge(r_step, base + steps[0])

                dve.wait_ge(router_mm, blk + 1)
                step(dve.tensor_scalar(vis_eps[:, :], banks[:, SB[0], BB:2 * BB], 1e-8, None, ALU.add))
                step(dve.reciprocal(vis_inv[:, :], vis_eps[:, :]))
                for h in range(2):
                    r = slice(h * T, h * T + T)
                    step(dve.tensor_tensor(ratio[r, :], banks[r, SB[0], h:BB:2], vis_inv[r, h:BB:2], ALU.mult))
                last = gw_last[:, :].rearrange("p (o e) -> p o e", o=1).to_broadcast((P, NP, NE))
                bias = gb[:, :].rearrange("p (o e) -> p o e", o=1).to_broadcast((P, NP, NE))
                step(dve.tensor_tensor(r_last[:, :, :], wide(ratio[:, :], NE), last, ALU.mult))
                step(dve.tensor_tensor(r_bias[:, :, :], r_last[:, :, :],
                                       banks[:, SB[1], 0:4 * NP].rearrange("p (n e) -> p n e", n=NP)[:, :, 0:NE],
                                       ALU.add))
                step(dve.tensor_tensor(logit[:, :, :], r_bias[:, :, :], bias, ALU.add))
                step(dve.tensor_reduce(l_max[:, :], logit[:, :, :], AX.X, ALU.max))
                step(dve.tensor_tensor(shifted[:, :, :], logit[:, :, :], wide(l_max[:, :], NE), ALU.subtract))
                assert steps[0] == R_SHIFT
                dve.wait_ge(router_exp, blk + 1)
                step(dve.tensor_reduce(e_sum[:, :], e_exp[:, :, :], AX.X, ALU.add))
                step(dve.reciprocal(e_inv[:, :], e_sum[:, :]))
                step(dve.tensor_tensor(score[:, :, :], e_exp[:, :, :], wide(e_inv[:, :], NE), ALU.mult))
                s0, s1, s2 = (score[:, :, e] for e in range(NE))
                step(dve.tensor_tensor(gt[:, 0, :], s1, s0, ALU.is_gt))
                step(dve.tensor_tensor(gt[:, 1, :], s2, s0, ALU.is_gt))
                step(dve.tensor_tensor(gt[:, 2, :], s2, s1, ALU.is_gt))
                step(dve.tensor_scalar(ngt[:, :, :], gt[:, :, :], -1.0, 1.0, ALU.mult, ALU.add))
                step(dve.tensor_tensor(rank[:, 0, :], gt[:, 0, :], gt[:, 1, :], ALU.add))
                step(dve.tensor_tensor(rank[:, 1, :], ngt[:, 0, :], gt[:, 2, :], ALU.add))
                step(dve.tensor_tensor(rank[:, 2, :], ngt[:, 1, :], ngt[:, 2, :], ALU.add))
                step(dve.tensor_scalar(pick[:, 0, :, :], rank[:, :, :], 0.0, None, ALU.is_equal))
                step(dve.tensor_scalar(pick[:, 1, :, :], rank[:, :, :], 1.0, None, ALU.is_equal))
                assert steps[0] == R_PICK
                return steps, step, s0, s1, s2

            def router_coefs(blk, state):
                steps, step, s0, s1, s2 = state
                step(dve.tensor_tensor(top[:, 0, :], s0, s1, ALU.max))
                step(dve.tensor_tensor(top[:, 1, :], s0, s1, ALU.min))
                step(dve.tensor_tensor(top[:, 2, :], top[:, 0, :], s2, ALU.min))
                step(dve.tensor_tensor(topn[:, 0, :], top[:, 0, :], s2, ALU.max))
                step(dve.tensor_tensor(topn[:, 1, :], top[:, 1, :], top[:, 2, :], ALU.max))
                step(dve.tensor_tensor(top[:, 3, :], topn[:, 0, :], topn[:, 1, :], ALU.add))
                step(dve.tensor_scalar(top[:, 4, :], top[:, 3, :], 1e-8, None, ALU.add))
                step(dve.reciprocal(top[:, 5, :], top[:, 4, :]))
                step(dve.tensor_tensor(top[:, 6:8, :], topn[:, :, :], top[:, 5:6, :].to_broadcast((P, 2, NP)),
                                       ALU.mult))
                dve.wait_ge(picked_mm, blk + 1)
                for i in range(2):
                    v = top[:, 6 + i:7 + i, :].to_broadcast((P, NE, NP))
                    w = slice(i * NE * NP, (i + 1) * NE * NP)
                    step(dve.tensor_tensor(part[:, i, :, :],
                                           banks[:, SB[0], w].rearrange("p (e n) -> p e n", e=NE), v, ALU.mult))
                step(dve.tensor_tensor(coef[:, :, :], part[:, 0, :, :], part[:, 1, :, :], ALU.add))
                assert steps[0] == R_STEPS
                flat = coef[:, :, :].rearrange("p e n -> p (e n)")
                dve.tensor_copy(coef_w[:, :, :, :].rearrange("p e n k -> p (e n) k"), wide(flat, P))\
                    .then_inc(coef_ready, 1)

            dve.sem_inc(w_lo, RING)
            for j in range(2):
                dve.sem_inc(drained[j], 1)
            dve.wait_ge(const_landed, 16 * N_CONST)
            dve.wait_ge(gwr_hi, 1)
            minus(gw_lo[:, :, :], gw[:, :, :], gw_hi[:, :, :]).then_inc(gwr_lo, 1)
            xh = b_hi[:, :, :].rearrange("p (n a) t -> p n (a t)", n=NP)
            xl = b_lo[:, :, :].rearrange("p (n a) t -> p n (a t)", n=NP)
            with dve.Fori(0, NBLK) as blk:
                dve.wait_ge(mixw_hi, blk + 1)
                minus(mix_lo[:, :, :], mix[:, :, :], mix_hi[:, :, :]).then_inc(mixw_lo, 1)
                for p in range(NP):
                    dve.wait_ge(x_hi, blk * NP + (p + 1))
                    minus(xl[:, p, :], x_nat[:, p, :], xh[:, p, :]).then_inc(x_lo, 1)
                lo_piece(blk, 0, 0)
                lo_piece(blk, 0, 1)
                for c in range(NC):
                    dve.wait_ge(h_hi, blk * NC + (c + 1))
                    minus(a_lo[:, c, :], banks[:, (SB + RB)[c % 4], :], a_hi[:, c, :]).then_inc(h_lo, 1)

                attention_slab(blk, 0, True)
                with dve.Fori(1, NC) as m:
                    attention_slab(blk, m, False)
                last = dve.snap(blk * NC + (NC - 1))
                softmax_scale(last)
                lo_piece(blk, G_O, 2)
                probs_lo(last)
                out_lo(last, NC - 1)

                dve.wait_ge(xT_landed, blk * 16 + 16)
                for n in range(NC):
                    dve.wait_ge(gemm_done, (blk * G_ALL + G_O) * RING + (n + 1))
                    dve.tensor_tensor(xT[:, n, :], banks[:, GB[n % 2], :], xT[:, n, :], ALU.add)\
                        .then_inc(drained[n % 2], 1)
                    if n > 0:
                        lo_piece(blk, G_O + (n + 2) // RING, (n + 2) % RING)
                    dve.wait_ge(x1_hi, blk * NC + (n + 1))
                    dve.wait_ge(drained[n % 2], blk * USES[n % 2] + (O_USE[n % 2] + n // 2 + 2))
                    minus(a_lo[:, n, :], xT[:, n, :], a_hi[:, n, :]).then_inc(x1_lo, 1)

                def y_turned(b):
                    dve.wait_ge(y_hi, blk * BB + (b + 1))
                    minus(b_lo[:, :, b * T:b * T + T],
                          banks[:, RB[b % 2], :].rearrange("p (c t) -> p c t", c=NC),
                          b_hi[:, :, b * T:b * T + T]).then_inc(y_lo, 1)

                for b in range(BB):
                    for c in range(NC):
                        lo_piece(blk, G_AD + 2 * b + (c + 2) // RING, (c + 2) % RING)
                        if c == 4 and b > 0:
                            y_turned(b - 1)
                y_turned(BB - 1)

                state = router_logits(blk)
                lo_piece(blk, G_FF, 2)
                router_coefs(blk, state)
                dve.wait_ge(coef_spread, blk + 1)

                def w1_piece(e, g, s, split_next=True):
                    n = e * 4 + g
                    k = O_USE[s % 2] + NC // 2 + s // 2
                    dve.wait_ge(drained[s % 2], blk * USES[s % 2] + (n * 2 + (k + 2)))
                    dve.tensor_tensor(scaled_t[:, s % 2, :], act_t[:, s % 2, :], banks[:, COEF_BANKS[e], :],
                                      ALU.mult).then_inc(act_scaled, 1)
                    if split_next:
                        lo_piece(blk, G_FF + n + (1 if s >= 2 else 0), (s + 2) % RING)
                    count = blk * (NE * NC) + (g * RING + (e * NC + s + 1))
                    dve.wait_ge(act_hi, count)
                    dve.wait_ge(act_scaled, count)
                    minus(a_lo[:, g * RING + s, :], scaled_t[:, s % 2, :], a_hi[:, g * RING + s, :])\
                        .then_inc(act_lo, 1)

                def w2_piece(e, g, s, more=True):
                    n = e * 4 + 2 + g
                    m = g * RING + s
                    if more:
                        lo_piece(blk, G_FF + n + (1 if s >= 2 else 0), (s + 2) % RING)
                    count = blk * (NE * NC) + (g * RING + (e * NC + s + 1))
                    dve.scalar_tensor_tensor(out=xT[:, m, :], in0=banks[:, COEF_BANKS[e], :],
                                             scalar=b2_t[:, e, bass.ds(m, 1)], in1=xT[:, m, :],
                                             op0=ALU.mult, op1=ALU.add).then_inc(bias_added, 1)
                    dve.wait_ge(gemm_done, (blk * G_ALL + (n + G_FF)) * RING + (s + 1))
                    dve.wait_ge(bias_added, count)
                    dve.tensor_tensor(xT[:, m, :], banks[:, GB[s % 2], :], xT[:, m, :], ALU.add)\
                        .then_inc(drained[s % 2], 1)

                for e in range(NE):
                    if e == 0:
                        for g in range(NC // RING):
                            for s in range(RING):
                                w1_piece(e, g, s, g > 0 or s > 0)
                    else:
                        with dve.Fori(0, NC // RING) as g:
                            for s in range(RING):
                                w1_piece(e, g, s)
                    if e < NE - 1:
                        with dve.Fori(0, NC // RING) as g:
                            for s in range(RING):
                                w2_piece(e, g, s)
                    else:
                        for s in range(RING):
                            w2_piece(e, 0, s)
                        for s in range(RING):
                            w2_piece(e, 1, s, s < 2)


def kernel(**inputs):
    import concourse.bacc as _bacc
    from concourse.bass_utils import run_bass_kernel_spmd as _run

    a = {k: np.asarray(v) for k, v in inputs.items()}

    def pieces(w):
        return np.ascontiguousarray(w.reshape(NC, P, NC, P).transpose(2, 1, 0, 3)).reshape(NC, P, D)

    def even_odd(w):
        return w.reshape(D, HEADS, DH // 2, 2).transpose(0, 1, 3, 2).reshape(D, D)

    x = a["x"].reshape(B * T, D)
    arrays = {
        "x_pairs": np.ascontiguousarray(x.reshape(NBLK, NP, P, D).transpose(0, 2, 1, 3)),
        "x_cols": np.ascontiguousarray(x.reshape(NBLK, BT, NC, P).transpose(0, 3, 2, 1)),
        "ids_mix": a["itok_B_0_15"].reshape(1, B),
        "ids_adapter": a["itok_B_1_14"].reshape(1, B),
        "mix_w": a["L0_cond_weights"],
        "wq": pieces(even_odd(a["L0_attn_Wq"])),
        "wk": pieces(even_odd(a["L0_attn_Wk"])),
        "wv": pieces(a["L0_attn_Wv"]),
        "wo": pieces(a["L0_attn_Wo"]),
        "adapter_w": np.ascontiguousarray(a["L0_cond2_weight"].transpose(0, 2, 1)).reshape(-1, P, D),
        "gate_w": np.ascontiguousarray(a["L0_ffn_gate_w"][:D].reshape(NC, P, NE).transpose(1, 0, 2)),
        "gate_last": a["L0_ffn_gate_w"][D:D + 1],
        "gate_b": a["L0_ffn_gate_b"].reshape(1, NE),
        "w1": np.concatenate([pieces(w) for w in a["L0_ffn_w1"]]),
        "b1": np.ascontiguousarray(a["L0_ffn_b1"].reshape(NE, NC, P).transpose(2, 0, 1)),
        "w2": np.concatenate([pieces(w) for w in a["L0_ffn_w2"]]),
        "b2": np.ascontiguousarray(a["L0_ffn_b2"].reshape(NE, NC, P).transpose(2, 0, 1)),
        "consts": shape_constants(),
    }
    nc = _bacc.Bacc("TRN2", target_bir_lowering=False, num_devices=1)
    args = [nc.dram_tensor(f"in_{n}", v.shape, mybir.dt.from_np(v.dtype), kind="ExternalInput").ap()
            for n, v in arrays.items()]
    args.append(nc.dram_tensor("out_0", (NBLK, P, NC, BT), F32, kind="ExternalOutput").ap())
    build(nc, *args)
    r = _run(nc, [{f"in_{n}": v for n, v in arrays.items()}], core_ids=[0])
    got = r.results[0]["out_0"]
    return np.ascontiguousarray(got.transpose(0, 3, 2, 1)).reshape(B, T, D)
```

```python
from contextlib import ExitStack

import numpy as np

import concourse.bass as bass
from concourse import mybir

F32 = mybir.dt.float32
F32R = mybir.dt.float32r
I32 = mybir.dt.int32
ALU = mybir.AluOpType
ACT = mybir.ActivationFunctionType
AX = mybir.AxisListType

P = 128
B, T, D = 32, 64, 1024
HEADS, DH = 16, 64
NE = 3
BT = 512
BB = BT // T
NBLK = B * T // BT
NC = D // P
NP = BT // P
RING = 4
GC = 8
VISION = int(T * 0.3)

WOVEN = ["q", 0, 1, "k", 2, 3, "v", 4, 5, 6, 7]
NW = len(WOVEN)
LAST = ["q", 0, 1, "k", 2, 3, 4, 5, 6, 7, "v"]
SLAB0 = RING
POS_O0 = NC * SLAB0
POS_IT = POS_O0 + NC
NF = NE * 2 * NC
POS_F = NC * NW
POS_FLAST = BB * NC
POS_O = POS_F + NF
POS_ALL = POS_O + NC
FILLS0 = (NC + NC // RING,) * 3 + (NC // RING,)
FILLS = POS_ALL // RING
USE_SLABS = (2 * NC, NC)
USE0 = tuple(u + NC // 2 for u in USE_SLABS)
USE_IT = tuple(u + NF // 2 + NC // 2 for u in USE_SLABS)
R_SHIFT, R_PICK, R_COEF, R_STEPS = 9, 21, 33, 44
SPAN0 = 4

C_ID, C_TWO, C_SEL, C_MASK, C_ROT, C_ONE, C_EIGHT, C_FROM, C_TO = 0, 128, 192, 320, 448, 512, 516, 520, 528
C_END = C_TO + BB


def shape_constants():
    c = np.zeros((P, C_END), np.float32)
    tok = np.arange(P)
    same = tok[:, None] // T == tok[None, :] // T
    c[:, C_ID:C_ID + P] = np.eye(P)
    c[:, C_TWO:C_TWO + T] = tok[:, None] % T == np.arange(T)[None, :]
    c[:, C_SEL:C_SEL + P] = same & (tok[:, None] % T == 0)
    c[:, C_MASK:C_MASK + P] = np.where(same & (tok[None, :] <= tok[:, None]), 0.0, -1e30)
    freq = 1.0 / 10000.0 ** (np.arange(0, DH, 2) / DH)
    angle = freq[:, None] * np.arange(T)[None, :]
    plus, minus = np.cos(angle) + np.sin(angle), np.cos(angle) - np.sin(angle)
    c[:, C_ROT:C_ROT + T] = np.concatenate([plus, minus, plus, minus])
    c[:, C_ONE] = 1.0
    c[:, C_EIGHT:C_EIGHT + 4] = tok[:, None] % 4 == np.arange(4)[None, :]
    c[:, C_FROM:C_FROM + BB] = BB - np.arange(BB)
    c[:, C_TO:C_TO + BB] = 1 + np.arange(BB)
    return c


def order(m):
    return WOVEN if m < NC - 1 else LAST


class Counts:

    def __init__(self, eng, i, last):
        fixed = isinstance(i, int)
        snap = (lambda v: v) if fixed else eng.snap
        self.i, self.last = i, last
        self.pos = snap(i * POS_ALL + POS_IT)
        self.fills = [snap(i * FILLS + FILLS0[s]) for s in (0, 3)]
        self.use = [snap(i * USE_IT[j] + USE0[j]) for j in range(2)]
        self.batch = snap(i * BB)
        self.slab = snap(i * NC + NC)
        self.act = snap(i * (NE * NC))
        self.f0 = POS_FLAST if last else POS_F
        self.fuse = (0, 0) if last else USE_SLABS

    def filled(self, off):
        return self.fills[off % RING == 3] + (off // RING + 1)


def build(nc, x_pairs, x_cols, ids_mix, ids_adapter, mix_w, wq, wk, wv, wo, adapter_w, gate_w,
          gate_last, gate_b, w1, b1, w2, b2, consts, out):
    ctx = ExitStack()
    with ctx:
        def sb(name, shape, dt=F32):
            return ctx.enter_context(nc.sbuf_tensor(name, shape, dt))

        def sem(name):
            return ctx.enter_context(nc.semaphore(name))

        raw = sb("raw", [P, RING, D])
        w_hi_t = sb("w_hi_t", [P, RING, D], F32R)
        w_lo_t = sb("w_lo_t", [P, RING, D], F32R)
        qk_land = sb("qk_land", [P, 2, NC, 2, 2, 32])
        ha_hi = sb("ha_hi", [P, NC, BT], F32R)
        ha_lo = sb("ha_lo", [P, NC, BT], F32R)
        ot_hi = sb("ot_hi", [P, NC, BT], F32R)
        ot_lo = sb("ot_lo", [P, NC, BT], F32R)
        yy = sb("yy", [P, NC, BB, 2, T], F32R)
        xT = sb("xT", [P, NC, BT])
        scratch = sb("scratch", [P, 4 * D])
        x_nat = scratch[:, :].rearrange("p (n d) -> p n d", n=NP)
        rot = scratch[:, 0:D].rearrange("p (j t) -> p j t", j=2)
        act_t = rot
        probs = scratch[:, D:2 * D].rearrange("p (h n k) -> p h n k", h=2, n=NP)
        scaled_t = scratch[:, D:2 * D].rearrange("p (j t) -> p j t", j=2)
        y_nat = scratch[:, 2 * D:3 * D]
        vT = scratch[:, 3 * D:3 * D + BT]
        spare = scratch[:, 3 * D + BT:4 * D]
        coef_w = scratch[:, 2 * D:2 * D + NE * NP * P].rearrange("p (e n k) -> p e n k", e=NE, n=NP)
        mix = qk_land[:, 1].rearrange("p c h u i -> p (c h u i)")[:, 0:NP * P].rearrange("p (n k) -> p n k", n=NP)
        qk_hi_t = sb("qk_hi_t", [P, 2, BT], F32R)
        qk_lo_t = sb("qk_lo_t", [P, 2, BT], F32R)
        v_hi_t = sb("v_hi_t", [P, NP, P], F32R)
        v_lo_t = sb("v_lo_t", [P, NP, P], F32R)
        mix_hi, mix_lo = v_hi_t, v_lo_t
        pt_hi_t = sb("pt_hi_t", [P, 2, BT], F32R)
        pt_lo_t = sb("pt_lo_t", [P, 2, BT], F32R)
        row_max = sb("row_max", [P, 2 * NP])
        row_sum = sb("row_sum", [P, 2 * NP])
        row_inv = sb("row_inv", [P, 2 * NP])
        junk = spare.rearrange("p (c t) -> p c t", c=NC)
        abs_sum_t = sb("abs_sum_t", [P, 2, BB])
        cst = sb("cst", [P, C_END])
        gw = sb("gw", [P, NC, NE])
        gw_two = sb("gw_two", [P, NC, GC], F32R)
        l_two = rot[0:8, 1, :]
        gw_last = sb("gw_last", [P, NE])
        gb = sb("gb", [P, NE])
        b1_t = sb("b1_t", [P, NE, NC])
        b2_t = sb("b2_t", [P, NE, NC])
        spans = sb("spans", [1, 2, NE], I32)
        idm = sb("idm", [1, B], I32)
        ida = sb("ida", [1, B], I32)
        taken = [0]

        def small(*dims):
            size = int(np.prod(dims))
            t = spare[:, taken[0]:taken[0] + size]
            taken[0] += size
            if len(dims) == 2:
                t = t.rearrange("p (a b) -> p a b", a=dims[0])
            if len(dims) == 3:
                t = t.rearrange("p (a b c) -> p a b c", a=dims[0], b=dims[1])
            return t

        vis_eps, vis_inv, ratio = small(BB), small(BB), small(NP)
        r_last, r_bias, logit, shifted, e_exp, score = (small(NP, NE) for _ in range(6))
        l_max, e_sum, e_inv = small(NP), small(NP), small(NP)
        gt, ngt, rank, pick = small(3, NP), small(3, NP), small(NE, NP), small(2, NE, NP)
        top, topn = small(8, NP), small(2, NP)
        part, coef = small(2, NE, NP), small(NE, NP)
        picked, used, first_in, last_in = small(2, 2, NE * NP), small(NE, NP, 2), small(NE, BB), small(NE, BB)
        s_from, s_to, s_sum, s_size, s_end = (small(NE) for _ in range(5))

        banks = ctx.enter_context(nc.psum_tensor("banks", [P, 8, 512], F32))
        GB = [0, 1]
        YB = [2, 3]
        TB = [4, 5]
        SB = [6, 7]
        MB = TB + SB
        CB = [SB[0], SB[1], YB[0]]
        ident = cst[:, C_ID:C_ID + P]

        def o_banks(pair):
            return banks[:, pair[0]:pair[1] + 1, :].rearrange("p a (n h t) -> p (a n) h t", n=2, h=2)


        const_landed = sem("const_landed")
        ids_landed = sem("ids_landed")
        mix_zeroed = sem("mix_zeroed")
        gw_zeroed = sem("gw_zeroed")
        raw_ready = [sem(f"raw_ready{s}") for s in range(RING)]
        qk_landed = [sem("q_landed"), sem("k_landed")]
        x_landed = sem("x_landed")
        mix_landed = sem("mix_landed")
        xT_landed = [sem("xT_landed0"), sem("xT_landed1")]
        w_hi = sem("w_hi")
        w_lo = sem("w_lo")
        x_hi, x_lo = sem("x_hi"), sem("x_lo")
        mixw_hi, mixw_lo = sem("mixw_hi"), sem("mixw_lo")
        gwr_hi, gwr_lo = sem("gwr_hi"), sem("gwr_lo")
        mixed = sem("mixed")
        h_hi, h_lo = sem("h_hi"), sem("h_lo")
        gemm_done = sem("gemm_done")
        drained = [sem("drained0"), sem("drained1")]
        qk_hi, qk_lo = sem("qk_hi"), sem("qk_lo")
        vt_done, v_hi, v_lo = sem("vt_done"), sem("v_hi"), sem("v_lo")
        score_done = sem("score_done")
        sm_mask, sm_max, sm_shift = sem("sm_mask"), sem("sm_max"), sem("sm_shift")
        sm_exp, sm_sum, sm_inv, sm_probs = sem("sm_exp"), sem("sm_sum"), sem("sm_inv"), sem("sm_probs")
        pt_done, pt_hi, pt_lo = sem("pt_done"), sem("pt_hi"), sem("pt_lo")
        pv_done, o_hi, o_lo = sem("pv_done"), sem("o_hi"), sem("o_lo")
        x1_hi, x1_lo = sem("x1_hi"), sem("x1_lo")
        y_copied, abs_summed = sem("y_copied"), sem("abs_summed")
        yt_done, y_hi, y_lo = sem("yt_done"), sem("y_hi"), sem("y_lo")
        lt_done, lt_copied = sem("lt_done"), sem("lt_copied")
        router_mm, router_exp, picked_mm = sem("router_mm"), sem("router_exp"), sem("picked_mm")
        r_step = sem("r_step")
        coef_ready, coef_spread = sem("coef_ready"), sem("coef_spread")
        spans_ready = sem("spans_ready")
        act_scaled, act_hi, act_lo = sem("act_scaled"), sem("act_hi"), sem("act_lo")
        bias_added = sem("bias_added")
        out_stored = [sem("out_stored0"), sem("out_stored1")]

        block = ctx.enter_context(nc.Block())
        N_CONST = 7
        HC = NC // 2

        def adapter_banks(k, b):
            return ((YB, SB)[b % 2], 2) if k.last else (YB, 1)

        def for_span(eng, k, e, body):
            first = eng.value_load(spans[0:1, 0, bass.ds(e, 1)], min_val=0, max_val=BB - SPAN0)
            size = eng.value_load(spans[0:1, 1, bass.ds(e, 1)], min_val=SPAN0, max_val=BB)
            for n in range(SPAN0, BB + 1):
                with eng.If(size == n):
                    body(nc.s_assert_within(first, 0, BB - n, skip_runtime_bounds_check_because=
                                            "the router keeps first + size within the block"), n)

        @block.sync
        def _(sp):
            def fill(pos, s, src):
                sp.wait_ge(w_hi, pos + 1)
                sp.wait_ge(w_lo, pos + 1)
                sp.dma_start(raw[:, s, :], src).then_inc(raw_ready[s], 16)

            def land(m, js=(0, 1)):
                for j, w in [(j, (wq, wk)[j]) for j in js]:
                    sp.dma_start(qk_land[:, j], w[m, :, :]).then_inc(qk_landed[j], 16)

            def load_mix(blk, zeroed):
                sp.wait_ge(mix_zeroed, zeroed)
                for b in range(BB):
                    a = sp.value_load(idm[0:1, bass.ds(blk * BB + b, 1)], min_val=0, max_val=15)
                    h = b % 2
                    sp.dma_start(mix[h * T:h * T + T, b // 2, h * T:h * T + T], mix_w[a, :, :])\
                      .then_inc(mix_landed, 16)

            def load_x(blk, zeroed):
                sp.dma_start(x_nat, x_pairs[blk, :, :, :]).then_inc(x_landed, 16)
                load_mix(blk, zeroed)

            sp.dma_start(idm[:, :], ids_mix).then_inc(ids_landed, 16)
            sp.dma_start(x_nat, x_pairs[0, :, :, :]).then_inc(x_landed, 16)
            sp.wait_ge(ids_landed, 16)
            load_mix(0, 1)
            sp.dma_start(ida[:, :], ids_adapter).then_inc(const_landed, 16)
            sp.dma_start(cst[:, :], consts).then_inc(const_landed, 16)
            sp.dma_start(gw[:, :, :], gate_w).then_inc(const_landed, 16)
            sp.dma_start(gw_last[:, :], gate_last.to_broadcast((P, NE))).then_inc(const_landed, 16)
            sp.dma_start(gb[:, :], gate_b.to_broadcast((P, NE))).then_inc(const_landed, 16)
            sp.dma_start(b1_t[:, :, :], b1).then_inc(const_landed, 16)
            sp.dma_start(b2_t[:, :, :], b2).then_inc(const_landed, 16)
            with sp.Fori(0, NC) as m:
                for j in range(2):
                    sp.wait_ge(w_hi, m * SLAB0 + (j + 1))
                    if j == 1:
                        sp.wait_ge(mixw_lo, 1)
                    land(m, (j,))
                fill(m * SLAB0 + 2, 2, wv[m, :, :])
            for n in range(6):
                fill(POS_O0 + n, n % RING, wo[n, :, :])
            sp.wait_ge(pt_done, 2 * NC)
            sp.wait_ge(vt_done, NC)
            load_x(1, 2)
            for n in range(6, NC):
                fill(POS_O0 + n, n % RING, wo[n, :, :])

            sp.wait_ge(const_landed, 16 * N_CONST)

            def iteration(i, last):
                if not last:
                    mixw = sp.snap(i + 2)
                k = Counts(sp, i, last)
                if not last:
                    land(0, (0,))
                    sp.wait_ge(mixw_lo, mixw)
                    land(0, (1,))
                for b in range(BB):
                    a = sp.value_load(ida[0:1, bass.ds(i * BB + b, 1)], min_val=0, max_val=15)
                    for w, piece in enumerate(range(NC) if last else order(b)):
                        off = b * (NC if last else NW) + w
                        if piece == "v":
                            fill(k.pos + off, off % RING, wv[b, :, :])
                            if b < NC - 1:
                                sp.wait_ge(w_hi, k.pos + (b * NW + WOVEN.index("k") + 1 + RING))
                                land(b + 1)
                        elif isinstance(piece, int):
                            fill(k.pos + off, off % RING, adapter_w[a * NC + piece, :, :])
                for e in range(NE):
                    for j, w in enumerate((w1, w2)):
                        with sp.Fori(0, NC // RING) as g:
                            for s in range(RING):
                                fill(k.pos + (g * RING + (k.f0 + (e * 2 + j) * NC + s)), s,
                                     w[g * RING + (e * NC + s), :, :])
                if not last:
                    with sp.If(i < NBLK - 2):
                        sp.wait_ge(act_lo, k.act + NE * NC)
                        blk = nc.s_assert_within(i + 2, 2, NBLK - 1, skip_runtime_bounds_check_because=
                                                 "the branch is taken only where i + 2 is a block")
                        load_x(blk, i + 3)
                    for n in range(NC):
                        fill(k.pos + (POS_O + n), n % RING, wo[n, :, :])

            with sp.Fori(0, NBLK - 1) as i:
                iteration(i, False)
            iteration(NBLK - 1, True)

        @block.gpsimd
        def _(pool):
            pool.memset(mix, 0.0).then_inc(mix_zeroed, 1)
            pool.memset(gw_two[:, :, :].bitcast(F32), 0.0).then_inc(gw_zeroed, 1)

            def take(j, slab, pos, s):
                r = raw[:, s, :].rearrange("p (c h u i) -> p c h u i", c=NC, h=2, u=2)
                even, odd = qk_land[:, j, :, :, 0, :], qk_land[:, j, :, :, 1, :]
                pool.wait_ge(qk_landed[j], slab * 16 + 16)
                pool.wait_ge(w_hi, pos + 1)
                pool.wait_ge(w_lo, pos + 1)
                pool.tensor_tensor(r[:, :, :, 0, :], even, odd, ALU.add)
                pool.tensor_tensor(r[:, :, :, 1, :], even, odd, ALU.subtract).then_inc(raw_ready[s], 16)

            def wide(t, k):
                return t.rearrange("p (n o) -> p n o", o=1).to_broadcast((P, t.shape[1], k))

            pr = probs.rearrange("p h n k -> p (h n) k")

            def softmax(slab):
                pool.wait_ge(sm_max, slab + 1)
                pool.tensor_tensor(pr, pr, wide(row_max[:, :], P), ALU.subtract).then_inc(sm_shift, 1)
                pool.wait_ge(sm_inv, slab + 1)
                pool.tensor_tensor(pr, pr, wide(row_inv[:, :], P), ALU.mult).then_inc(sm_probs, 1)

            def zero_mix():
                pool.memset(mix, 0.0).then_inc(mix_zeroed, 1)

            for j in range(2):
                take(j, 0, j, j)
            for h in range(2):
                c = slice(h * HC, h * HC + HC)
                pool.dma_start(xT[:, c, :], x_cols[0, :, c, :]).then_inc(xT_landed[h], 16)
            with pool.Fori(0, NC - 1) as m:
                for j in range(2):
                    take(j, m + 1, m * SLAB0 + (SLAB0 + j), j)
                softmax(m)
            softmax(NC - 1)
            zero_mix()

            def iteration(i, last):
                k = Counts(pool, i, last)
                if not last:
                    for m in range(NC):
                        for j, what in enumerate("qk"):
                            off = m * NW + order(m).index(what)
                            take(j, k.slab + m, k.pos + off, off % RING)
                        if m > 0:
                            softmax(k.slab + (m - 1))
                    softmax(k.slab + (NC - 1))
                    zero_mix()
                for n in range(NC):
                    use = k.fuse[n % 2] + NF // 2 - NC // 2 + n // 2
                    done = k.use[n % 2] + (use + 2)
                    if not last:
                        done = pool.snap(done)
                    pool.wait_ge(drained[n % 2], done)
                    pool.dma_start(out[i, :, n, :], xT[:, n, :]).then_inc(out_stored[n // HC], 16)
                    if not last and n in (HC, NC - 1):
                        h = int(n == NC - 1)
                        c = slice(h * HC, h * HC + HC)
                        pool.wait_ge(out_stored[h], i * (16 * HC) + 16 * HC)
                        pool.dma_start(xT[:, c, :], x_cols[i + 1, :, c, :]).then_inc(xT_landed[h], 16)

            with pool.Fori(0, NBLK - 1) as i:
                iteration(i, False)
            iteration(NBLK - 1, True)
            for h in range(2):
                pool.wait_ge(out_stored[h], 16 * HC * NBLK)

        @block.tensor
        def _(pe):
            def three(dst, l_hi, l_lo, r_hi, r_lo, start, stop):
                pe.matmul(dst, l_hi, r_hi, start=start, stop=False)
                pe.matmul(dst, l_hi, r_lo, start=False, stop=False)
                return pe.matmul(dst, l_lo, r_hi, start=False, stop=stop)

            def wait_piece(pos):
                pe.wait_ge(w_hi, pos + (1 + RING))
                pe.wait_ge(w_lo, pos + (1 + RING))

            def moving(src, c, span):
                first, n = span
                if src == "yy":
                    return yy[:, c, bass.ds(first, n), 0, :], yy[:, c, bass.ds(first, n), 1, :]
                hi, lo = {"ha": (ha_hi, ha_lo), "ot": (ot_hi, ot_lo)}[src]
                return hi[:, c, bass.ds(first * T, n * T)], lo[:, c, bass.ds(first * T, n * T)]

            def chunks(s, bank, src, cs, ready=None, span=(0, BB)):
                dst = banks[:, bank, bass.ds(span[0] * T, span[1] * T)]
                if src == "yy":
                    dst = dst.rearrange("p (b t) -> p b t", b=span[1])
                for c in cs:
                    if ready is not None:
                        ready_hi, ready_lo, base = ready
                        pe.wait_ge(ready_hi, base + (c + 1))
                        pe.wait_ge(ready_lo, base + (c + 1))
                    w = slice(c * P, c * P + P)
                    hi, lo = moving(src, c, span)
                    mm = three(dst, w_hi_t[:, s, w], w_lo_t[:, s, w], hi, lo, c == 0, c == NC - 1)
                return mm

            def gemm(pos, s, bank, use, src, ready=None, n=1, span=(0, BB)):
                wait_piece(pos)
                pe.wait_ge(drained[bank], use + 1)
                chunks(s, GB[bank], src, range(NC), ready, span).then_inc(gemm_done, n)

            def mix_tokens(blk):
                pe.wait_ge(mixw_hi, blk + 1)
                pe.wait_ge(mixw_lo, blk + 1)
                pe.wait_ge(x_hi, blk * NP + NP)
                pe.wait_ge(x_lo, blk * NP + NP)
                for c in range(NC):
                    if c >= len(MB):
                        pe.wait_ge(h_hi, blk * NC + (c - 3))
                        pe.wait_ge(h_lo, blk * NC + (c - 3))
                    for p in range(NP):
                        w = slice(p * P, p * P + P)
                        mm = three(banks[:, MB[c % 4], w], ha_hi[:, c, w], ha_lo[:, c, w],
                                   mix_hi[:, p, :], mix_lo[:, p, :], True, True)
                    mm.then_inc(mixed, 1)

            def turn_probs(slab):
                pe.wait_ge(sm_probs, slab + 1)
                pe.wait_ge(v_hi, slab + 1)
                pe.wait_ge(v_lo, slab + 1)
                for h in range(2):
                    for p in range(NP):
                        mm = pe.transpose(banks[:, TB[h], p * P:p * P + P], probs[:, h, p, :], ident)
                    mm.then_inc(pt_done, 1)

            def outputs(slab, pair):
                pe.wait_ge(pt_hi, slab * 2 + 2)
                pe.wait_ge(pt_lo, slab * 2 + 2)
                for p in range(NP):
                    w = slice(p * P, p * P + P)
                    dst = banks[:, pair[p // 2], p % 2 * 2 * P:(p % 2 + 1) * 2 * P].rearrange("p (h t) -> p h t", h=2)
                    mm = three(dst, v_hi_t[:, p, :], v_lo_t[:, p, :], pt_hi_t[:, :, w], pt_lo_t[:, :, w],
                               True, True)
                mm.then_inc(pv_done, 1)

            def turn_values(copied):
                pe.wait_ge(drained[0], copied)
                for p in range(NP):
                    w = slice(p * P, p * P + P)
                    mm = pe.transpose(banks[:, TB[0], w], vT[:, w], ident)
                mm.then_inc(vt_done, 1)

            def scores(slab):
                pe.wait_ge(qk_hi, slab * 2 + 2)
                pe.wait_ge(qk_lo, slab * 2 + 2)
                for p in range(NP):
                    for h in range(2):
                        w, r = slice(p * P, p * P + P), slice(h * DH, h * DH + DH)
                        mm = three(banks[:, SB[h], w], qk_hi_t[r, 0, w], qk_lo_t[r, 0, w],
                                   qk_hi_t[r, 1, w], qk_lo_t[r, 1, w], True, True)
                mm.then_inc(score_done, 1)

            def adapter_piece(k, b, c, off):
                wait_piece(k.pos + off)
                if b == 0:
                    pe.wait_ge(x1_hi, k.batch + (c + 1))
                    pe.wait_ge(x1_lo, k.batch + (c + 1))
                pair, lag = adapter_banks(k, b)
                if c == 0 and b >= lag:
                    pe.wait_ge(y_copied, k.batch + (b - lag + 1))
                still = yy[:, c, b, :, :].rearrange("p u t -> p (u t)")
                for half in range(2):
                    w = slice(half * 512, half * 512 + 512)
                    pe.matmul(banks[:, pair[half], :], still, w_hi_t[:, off % RING, w],
                              start=(c == 0), stop=False)
                    mm = pe.matmul(banks[:, pair[half], :], still, w_lo_t[:, off % RING, w],
                                   start=False, stop=(c == NC - 1))
                mm.then_inc(gemm_done, 1)

            def turn_y(k, b):
                pe.wait_ge(y_copied, k.batch + (b + 1))
                if b > 0:
                    wait_turned(k, b - 1)
                for c in range(NC):
                    mm = pe.matmul(banks[:, TB[1], c * T:c * T + T], y_nat[:, c * P:c * P + P],
                                   cst[:, C_TWO:C_TWO + T], start=True, stop=True)
                mm.then_inc(yt_done, 1)

            def wait_turned(k, b):
                pe.wait_ge(y_hi, k.batch + (b + 1))
                pe.wait_ge(y_lo, k.batch + (b + 1))
                pe.wait_ge(abs_summed, k.batch + (b + 1))

            def project(pos0, use, n, ready=None):
                gemm(pos0 + n, n % RING, n % 2, use[n % 2] + n // 2, "ot", ready)

            ones = cst[:, C_ONE:C_ONE + 1].to_broadcast((P, P))

            def plain_slab(m, first):
                pos = m * SLAB0
                gemm(pos, 0, 0, m * 2, "ha", (h_hi, h_lo, 0) if first else None)
                gemm(pos + 1, 1, 1, m, "ha")
                if not first:
                    turn_probs(m - 1)
                gemm(pos + 2, 2, 0, m * 2 + 1, "ha", n=2)
                if not first:
                    outputs(m - 1, YB)
                turn_values(m * 2 + 3)
                scores(m)

            mix_tokens(0)
            pe.wait_ge(const_landed, 16 * N_CONST)
            pe.wait_ge(gwr_hi, 1)
            pe.wait_ge(gwr_lo, 1)
            plain_slab(0, True)
            with pe.Fori(1, NC) as m:
                plain_slab(m, False)
            for n in range(2):
                wait_piece(POS_O0 + n)
                pe.wait_ge(drained[n], USE_SLABS[n] + 1)
                chunks(n, GB[n], "ot", range(NC - 1), (o_hi, o_lo, 0) if n == 0 else None)
            turn_probs(NC - 1)
            outputs(NC - 1, YB)
            for n in range(2):
                chunks(n, GB[n], "ot", [NC - 1], (o_hi, o_lo, 0)).then_inc(gemm_done, 1)
            for n in range(2, NC):
                project(POS_O0, USE_SLABS, n)

            def woven_slab(k, m):
                slab = k.slab + m
                for w, piece in enumerate(order(m)):
                    off = m * NW + w
                    if piece == "q":
                        gemm(k.pos + off, off % RING, 0, k.use[0] + 2 * m, "ha",
                             (h_hi, h_lo, k.batch + NC) if m == 0 else None)
                    elif piece == "k":
                        gemm(k.pos + off, off % RING, 1, k.use[1] + m, "ha")
                        if m > 0:
                            if m > 1:
                                wait_turned(k, m - 2)
                            turn_probs(slab - 1)
                    elif piece == "v":
                        gemm(k.pos + off, off % RING, 0, k.use[0] + (2 * m + 1), "ha")
                        if m > 0:
                            outputs(slab - 1, SB)
                        if m == NC - 1:
                            turn_y(k, m)
                            turn_values(k.use[0] + (2 * m + 3))
                    else:
                        adapter_piece(k, m, piece, off)
                        if piece == 4 and m < NC - 1:
                            turn_values(k.use[0] + (2 * m + 3))
                        if piece == 5 and m > 0:
                            turn_y(k, m - 1)
                if m > 0:
                    pe.wait_ge(o_hi, slab)
                    pe.wait_ge(o_lo, slab)
                scores(slab)

            def expert_piece(k, f, g, ready=None, span=(0, BB)):
                src = "ha" if f // NC % 2 else "yy"
                gemm(k.pos + (g * RING + (k.f0 + f)), f % RING, f % 2,
                     k.use[f % 2] + (g * 2 + (k.fuse[f % 2] + f // 2)), src, ready, 1, span)

            def experts(k):
                if k.last:
                    turn_y(k, BB - 1)
                pe.wait_ge(y_hi, k.batch + BB)
                pe.wait_ge(y_lo, k.batch + BB)
                dst = banks[0:GC, YB[0], :].rearrange("p (b t) -> p b t", b=BB)
                for c in range(NC):
                    for u in range(2):
                        mm = pe.matmul(dst, gw_two[:, c, :], yy[:, c, :, u, :],
                                       start=(c == 0 and u == 0), stop=(c == NC - 1 and u == 1))
                mm.then_inc(lt_done, 1)
                expert_piece(k, 0, 0)
                pe.wait_ge(abs_summed, k.batch + BB)
                pe.matmul(banks[:, YB[1], 0:BB], ones, abs_sum_t[:, 0, :],
                          start=True, stop=True)
                pe.matmul(banks[:, YB[1], BB:2 * BB], ones, abs_sum_t[:, 1, :],
                          start=True, stop=True)
                pe.wait_ge(lt_copied, k.i + 1)
                for p in range(NP):
                    mm = pe.matmul(banks[:, YB[1], 32 + 4 * p:36 + 4 * p], l_two[:, p * P:p * P + P],
                                   cst[0:8, C_EIGHT:C_EIGHT + 4], start=True, stop=True)
                mm.then_inc(router_mm, 1)
                if not k.last:
                    wait_turned(k, BB - 1)
                    turn_probs(k.slab + (NC - 1))
                expert_piece(k, 1, 0)
                if not k.last:
                    outputs(k.slab + (NC - 1), SB)
                picks = pick[:, :, :, :].rearrange("p a e n -> p (a e n)")
                pe.wait_ge(r_step, k.i * R_STEPS + R_PICK)
                pe.matmul(banks[:, YB[1], 64:64 + 2 * NE * NP], cst[:, C_SEL:C_SEL + P],
                          picks, start=True, stop=True)
                for h in range(2):
                    w = slice(128 + h * 2 * NE * NP, 128 + (h + 1) * 2 * NE * NP)
                    mm = pe.matmul(banks[:, YB[1], w], cst[:, C_SEL + h * T:C_SEL + h * T + 1].to_broadcast((P, P)),
                                   picks, start=True, stop=True)
                mm.then_inc(picked_mm, 1)
                expert_piece(k, 2, 0)
                pe.wait_ge(coef_ready, k.i + 1)
                if not k.last:
                    pe.wait_ge(o_hi, k.slab + NC)
                    pe.wait_ge(o_lo, k.slab + NC)
                for e in range(NE):
                    for p in range(NP):
                        mm = pe.matmul(banks[:, CB[e], p * P:p * P + P], coef_w[:, e, p, :],
                                       ident, start=True, stop=True)
                mm.then_inc(coef_spread, 1)
                pe.wait_ge(spans_ready, k.i + 1)
                for f in range(3, NC):
                    expert_piece(k, f, 0)
                for e in range(NE):
                    def pieces(first, n):
                        for j in range(int(e == 0), 2):
                            with pe.Fori(0, NC // RING) as g:
                                for s in range(RING):
                                    expert_piece(k, (e * 2 + j) * NC + s, g,
                                                 (act_hi, act_lo, k.act + e * NC) if s == 0 and j == 1 else None,
                                                 (first, n))

                    for_span(pe, k, e, pieces)

            def iteration(i, last):
                k = Counts(pe, i, last)
                if last:
                    for b in range(BB):
                        for c in range(NC):
                            adapter_piece(k, b, c, b * NC + c)
                            if c == 3 and b > 0:
                                turn_y(k, b - 1)
                    experts(k)
                    return
                mix_tokens(i + 1)
                for m in range(NC):
                    woven_slab(k, m)
                experts(k)
                for n in range(NC):
                    project(k.pos + POS_O, [k.use[j] + (USE_SLABS[j] + NF // 2) for j in range(2)], n)

            with pe.Fori(0, NBLK - 1) as i:
                iteration(i, False)
            iteration(NBLK - 1, True)

        @block.scalar
        def _(act):
            def copy(dst, src):
                return act.activation(dst, src, ACT.Copy)

            def split(pos, s, filled, n=1):
                act.wait_ge(raw_ready[s], filled * 16)
                if not (isinstance(pos, int) and pos < RING):
                    act.wait_ge(gemm_done, pos - (RING - 1))
                copy(w_hi_t[:, s, :], raw[:, s, :]).then_inc(w_hi, n)

            def split_x(blk):
                act.wait_ge(x_landed, blk * 16 + 16)
                for p in range(NP):
                    copy(ha_hi[:, :, p * P:p * P + P], x_nat[:, p, :].rearrange("p (c d) -> p c d", c=NC))\
                        .then_inc(x_hi, 1)
                act.wait_ge(mix_landed, blk * (16 * BB) + 16 * BB)
                copy(mix_hi[:, :, :], mix).then_inc(mixw_hi, 1)

            def mixed_hi(blk):
                for c in range(NC):
                    act.wait_ge(mixed, blk * NC + (c + 1))
                    copy(ha_hi[:, c, :], banks[:, MB[c % 4], :]).then_inc(h_hi, 1)

            def rotated_hi(slab, j, rotated):
                act.wait_ge(drained[j], rotated)
                copy(qk_hi_t[:, j, :], rot[:, j, :]).then_inc(qk_hi, 1)

            def exp(slab):
                act.wait_ge(sm_shift, slab + 1)
                act.activation(probs, probs, ACT.Exp).then_inc(sm_exp, 1)

            def probs_hi(slab):
                for h in range(2):
                    act.wait_ge(pt_done, slab * 2 + (h + 1))
                    copy(pt_hi_t[:, h, :], banks[:, TB[h], :]).then_inc(pt_hi, 1)

            def copy_values(done):
                act.wait_ge(gemm_done, done)
                copy(vT, banks[:, GB[0], :]).then_inc(drained[0], 1)

            def values_hi(slab):
                act.wait_ge(vt_done, slab + 1)
                copy(v_hi_t[:, :, :].rearrange("p n k -> p (n k)"), banks[:, TB[0], :]).then_inc(v_hi, 1)

            def out_hi(slab, m, pair):
                act.wait_ge(pv_done, slab + 1)
                for h in range(2):
                    r = slice(h * DH, h * DH + DH)
                    ins = copy(ot_hi[r, m, :].rearrange("p (n t) -> p n t", n=NP), o_banks(pair)[r, :, h, :])
                ins.then_inc(o_hi, 1)

            def x1_piece(batch, n, added):
                act.wait_ge(drained[n % 2], added)
                copy(yy[:, n, :, 0, :], xT[:, n, :].rearrange("p (b t) -> p b t", b=BB)).then_inc(x1_hi, 1)

            def copy_y(k, b, done):
                act.wait_ge(gemm_done, done)
                pair, _ = adapter_banks(k, b)
                copy(y_nat, banks[:, pair[0]:pair[0] + 2, :].rearrange("p a n -> p (a n)")).then_inc(y_copied, 1)

            def turned_y(k, b):
                act.wait_ge(yt_done, k.batch + (b + 1))
                yt = banks[:, TB[1], :].rearrange("p (c t) -> p c t", c=NC)
                copy(yy[:, :, b, 0, :], yt).then_inc(y_hi, 1)
                for u, t in enumerate((slice(VISION, T), slice(0, VISION))):
                    ins = act.activation(junk[:, :, t], yt[:, :, t], ACT.Abs, accum_out=abs_sum_t[:, u, b:b + 1])
                ins.then_inc(abs_summed, 1)

            act.sem_inc(w_hi, RING)

            def plain_slab(m, first):
                split(m * SLAB0 + 2, 2, m + 1, 2)
                if not first:
                    exp(m - 1)
                rotated_hi(m, 0, m * 2 + 2)
                rotated_hi(m, 1, m + 2)
                if not first:
                    probs_hi(m - 1)
                split(m * SLAB0 + SLAB0, 0, m + 2)
                copy_values(m * SLAB0 + 4)
                if not first:
                    out_hi(m - 1, m - 1, YB)
                split(m * SLAB0 + (SLAB0 + 1), 1, m + 2)
                values_hi(m)

            split_x(0)
            split(0, 0, 1)
            split(1, 1, 1)
            mixed_hi(0)
            act.wait_ge(const_landed, 16 * N_CONST)
            act.wait_ge(gw_zeroed, 1)
            copy(gw_two[:, :, 0:NE], gw[:, :, :]).then_inc(gwr_hi, 1)
            plain_slab(0, True)
            with act.Fori(1, NC) as m:
                plain_slab(m, False)
            exp(NC - 1)
            split(POS_O0 + 2, 2, FILLS0[2] - 1)
            probs_hi(NC - 1)
            out_hi(NC - 1, NC - 1, YB)
            k0 = Counts(act, 0, False)

            def project_piece(pos, filled, n, batch, use):
                split(pos, (n + 3) % RING, filled)
                x1_piece(batch, n, use[n % 2] + (n // 2 + 2))

            for n in range(NC):
                off = n + 3 - NC
                filled = k0.filled(off) if off >= 0 else FILLS0[(n + 3) % RING] - (1 if off < -RING else 0)
                project_piece(POS_IT + off, filled, n, 0, USE_SLABS)
                if n == 3:
                    split_x(1)

            def experts(k):
                def split_ahead(f, g=0):
                    off = k.f0 + f + 3
                    split(k.pos + (g * RING + off), off % RING, k.filled(off) + g)

                def activate(e, f, g, func):
                    act.wait_ge(gemm_done, k.pos + (g * RING + (k.f0 + f + 1)))
                    act.activation(act_t[:, f % 2, :], banks[:, GB[f % 2], :], func,
                                   bias=b1_t[:, e, bass.ds(g * RING + f % NC, 1)])\
                        .then_inc(drained[f % 2], 1)

                def scaled_hi(e, m, g):
                    act.wait_ge(act_scaled, k.act + (g * RING + (e * NC + m + 1)))
                    copy(ha_hi[:, g * RING + m, :], scaled_t[:, m % 2, :]).then_inc(act_hi, 1)

                if k.last:
                    copy_y(k, BB - 1, k.pos + k.f0)
                    turned_y(k, BB - 1)
                else:
                    exp(k.slab + (NC - 1))
                act.wait_ge(lt_done, k.i + 1)
                copy(l_two[:, :], banks[0:8, YB[0], :]).then_inc(lt_copied, 1)
                split_ahead(0)
                activate(0, 0, 0, ACT.Tanh)
                if not k.last:
                    probs_hi(k.slab + (NC - 1))
                split_ahead(1)
                act.wait_ge(r_step, k.i * R_STEPS + R_SHIFT)
                act.activation(e_exp[:, :, :], shifted[:, :, :], ACT.Exp).then_inc(router_exp, 1)
                activate(0, 1, 0, ACT.Tanh)
                if not k.last:
                    out_hi(k.slab + (NC - 1), NC - 1, SB)
                split_ahead(2)
                for m in range(2):
                    scaled_hi(0, m, 0)
                activate(0, 2, 0, ACT.Tanh)
                scaled_hi(0, 2, 0)
                for m in range(3, NC):
                    split_ahead(m)
                    activate(0, m, 0, ACT.Tanh)
                    scaled_hi(0, m, 0)
                for e, func in enumerate((ACT.Tanh, ACT.Gelu, ACT.Silu)):
                    if e > 0:
                        with act.Fori(0, NC // RING) as g:
                            for s in range(RING):
                                split_ahead(e * 2 * NC + s, g)
                                activate(e, e * 2 * NC + s, g, func)
                                scaled_hi(e, s, g)
                    if e < NE - 1 or not k.last:
                        with act.Fori(0, NC // RING) as g:
                            for s in range(RING):
                                split_ahead((e * 2 + 1) * NC + s, g)
                    else:
                        for m in range(NC - 3):
                            split_ahead((e * 2 + 1) * NC + m)

            def iteration(i, last):
                k = Counts(act, i, last)

                def ahead(off):
                    split(k.pos + (off + 3), (off + 3) % RING, k.filled(off + 3))

                if last:
                    for b in range(BB):
                        for c in range(NC):
                            ahead(b * NC + c) if c or not b else None
                            if c == 0 and b > 0:
                                copy_y(k, b - 1, k.pos + b * NC)
                                ahead(b * NC + c)
                            if c == 4 and b > 0:
                                turned_y(k, b - 1)
                    experts(k)
                    return
                mixed_hi(i + 1)
                for m in range(NC):
                    slab = k.slab + m
                    for w, piece in enumerate(order(m)):
                        off = m * NW + w
                        if piece == "q":
                            if m > 0:
                                copy_y(k, m - 1, k.pos + off)
                            ahead(off)
                            if m > 0:
                                exp(slab - 1)
                            rotated_hi(slab, 0, k.use[0] + (2 * m + 2))
                        elif piece == "k":
                            ahead(off)
                            rotated_hi(slab, 1, k.use[1] + (m + 2))
                            if m > 0:
                                probs_hi(slab - 1)
                        elif piece == "v":
                            if m == NC - 1:
                                copy_y(k, m, k.pos + off)
                            ahead(off)
                            copy_values(k.pos + (off + 1))
                            if m > 0:
                                out_hi(slab - 1, m - 1, SB)
                            if m == NC - 1:
                                turned_y(k, m)
                                values_hi(slab)
                        else:
                            ahead(off)
                            if piece == 4 and m < NC - 1:
                                values_hi(slab)
                            if piece == 6 and m > 0:
                                turned_y(k, m - 1)
                experts(k)
                for n in range(NC):
                    off = POS_O + n + 3
                    project_piece(k.pos + off, k.filled(off), n, k.slab,
                                  [k.use[j] + (USE_SLABS[j] + NF // 2) for j in range(2)])
                    if n == 3:
                        with act.If(i < NBLK - 2):
                            split_x(i + 2)

            with act.Fori(0, NBLK - 1) as i:
                iteration(i, False)
            iteration(NBLK - 1, True)

        @block.vector
        def _(dve):
            def minus(dst, src, hi):
                return dve.tensor_tensor(dst, src, hi.bitcast(F32), ALU.subtract)

            def lo_piece(pos, s, n=1):
                dve.wait_ge(w_hi, pos + (1 + RING))
                minus(w_lo_t[:, s, :], raw[:, s, :], w_hi_t[:, s, :]).then_inc(w_lo, n)

            rot_f = cst[:, C_ROT:C_ROT + T].rearrange("p (o t) -> p o t", o=1).to_broadcast((P, BB, T))
            mask = cst[:, C_MASK:C_MASK + P].rearrange("p (o t) -> p o t", o=1).to_broadcast((P, NP, P))

            def wide(t, k):
                return t.rearrange("p (n o) -> p n o", o=1).to_broadcast((P, t.shape[1], k))

            def split_x(blk):
                for p in range(NP):
                    w = slice(p * P, p * P + P)
                    dve.wait_ge(x_hi, blk * NP + (p + 1))
                    minus(ha_lo[:, :, w], x_nat[:, p, :].rearrange("p (c d) -> p c d", c=NC),
                          ha_hi[:, :, w]).then_inc(x_lo, 1)
                dve.wait_ge(mixw_hi, blk + 1)
                minus(mix_lo[:, :, :], mix, mix_hi[:, :, :]).then_inc(mixw_lo, 1)

            def mixed_lo(blk):
                for c in range(NC):
                    dve.wait_ge(h_hi, blk * NC + (c + 1))
                    minus(ha_lo[:, c, :], banks[:, MB[c % 4], :], ha_hi[:, c, :]).then_inc(h_lo, 1)

            def rotate(j, done):
                dve.wait_ge(gemm_done, done)
                dve.tensor_tensor(rot[:, j, :].rearrange("p (b t) -> p b t", b=BB),
                                  banks[:, GB[j], :].rearrange("p (b t) -> p b t", b=BB), rot_f, ALU.mult)\
                    .then_inc(drained[j], 1)

            def rotated_lo(slab, j, rotated):
                dve.wait_ge(qk_hi, slab * 2 + (j + 1))
                dve.wait_ge(drained[j], rotated)
                minus(qk_lo_t[:, j, :], rot[:, j, :], qk_hi_t[:, j, :]).then_inc(qk_lo, 1)

            pr = probs.rearrange("p h n k -> p (h n) k")

            def softmax_max(slab):
                dve.wait_ge(score_done, slab + 1)
                for h in range(2):
                    dve.scalar_tensor_tensor(
                        out=probs[:, h, :, :], in0=banks[:, SB[h], :].rearrange("p (n k) -> p n k", n=NP),
                        scalar=0.5 / DH ** 0.5, in1=mask, op0=ALU.mult, op1=ALU.add).then_inc(sm_mask, 1)
                dve.wait_ge(sm_mask, slab * 2 + 2)
                dve.tensor_reduce(row_max[:, :], pr, AX.X, ALU.max).then_inc(sm_max, 1)

            def softmax_sum(slab):
                dve.wait_ge(sm_exp, slab + 1)
                dve.tensor_reduce(row_sum[:, :], pr, AX.X, ALU.add).then_inc(sm_sum, 1)
                dve.wait_ge(sm_sum, slab + 1)
                dve.reciprocal(row_inv[:, :], row_sum[:, :]).then_inc(sm_inv, 1)

            def probs_lo(slab):
                for h in range(2):
                    dve.wait_ge(pt_hi, slab * 2 + (h + 1))
                    minus(pt_lo_t[:, h, :], banks[:, TB[h], :], pt_hi_t[:, h, :]).then_inc(pt_lo, 1)

            def values_lo(slab):
                dve.wait_ge(v_hi, slab + 1)
                minus(v_lo_t[:, :, :].rearrange("p n k -> p (n k)"), banks[:, TB[0], :],
                      v_hi_t[:, :, :].rearrange("p n k -> p (n k)")).then_inc(v_lo, 1)

            def out_lo(slab, m, pair):
                dve.wait_ge(o_hi, slab + 1)
                for h in range(2):
                    r = slice(h * DH, h * DH + DH)
                    ins = minus(ot_lo[r, m, :].rearrange("p (n t) -> p n t", n=NP), o_banks(pair)[r, :, h, :],
                                ot_hi[r, m, :].rearrange("p (n t) -> p n t", n=NP))
                ins.then_inc(o_lo, 1)

            def turned_y(k, b):
                dve.wait_ge(y_hi, k.batch + (b + 1))
                dve.wait_ge(abs_summed, k.batch + (b + 1))
                minus(yy[:, :, b, 1, :], banks[:, TB[1], :].rearrange("p (c t) -> p c t", c=NC),
                      yy[:, :, b, 0, :]).then_inc(y_lo, 1)

            def router(k):
                base = k.i * R_STEPS if isinstance(k.i, int) else dve.snap(k.i * R_STEPS)
                steps = [0]

                def step(ins):
                    ins.then_inc(r_step, 1)
                    steps[0] += 1
                    dve.wait_ge(r_step, base + steps[0])

                dve.wait_ge(router_mm, k.i + 1)
                step(dve.tensor_scalar(vis_eps[:, :], banks[:, YB[1], BB:2 * BB], 1.0 / (VISION * D), 1e-8,
                                       ALU.mult, ALU.add))
                step(dve.reciprocal(vis_inv[:, :], vis_eps[:, :]))
                for h in range(2):
                    r = slice(h * T, h * T + T)
                    step(dve.scalar_tensor_tensor(out=ratio[r, :], in0=banks[r, YB[1], h:BB:2],
                                                  scalar=1.0 / ((T - VISION) * D), in1=vis_inv[r, h:BB:2],
                                                  op0=ALU.mult, op1=ALU.mult))
                last = gw_last[:, :].rearrange("p (o e) -> p o e", o=1).to_broadcast((P, NP, NE))
                bias = gb[:, :].rearrange("p (o e) -> p o e", o=1).to_broadcast((P, NP, NE))
                rows = banks[:, YB[1], 32:32 + 4 * NP].rearrange("p (n e) -> p n e", n=NP)[:, :, 0:NE]
                step(dve.tensor_tensor(r_last[:, :, :], wide(ratio[:, :], NE), last, ALU.mult))
                step(dve.tensor_tensor(r_bias[:, :, :], r_last[:, :, :], rows, ALU.add))
                step(dve.tensor_tensor(logit[:, :, :], r_bias[:, :, :], bias, ALU.add))
                step(dve.tensor_reduce(l_max[:, :], logit[:, :, :], AX.X, ALU.max))
                step(dve.tensor_tensor(shifted[:, :, :], logit[:, :, :], wide(l_max[:, :], NE), ALU.subtract))
                assert steps[0] == R_SHIFT
                yield
                dve.wait_ge(router_exp, k.i + 1)
                step(dve.tensor_reduce(e_sum[:, :], e_exp[:, :, :], AX.X, ALU.add))
                step(dve.reciprocal(e_inv[:, :], e_sum[:, :]))
                step(dve.tensor_tensor(score[:, :, :], e_exp[:, :, :], wide(e_inv[:, :], NE), ALU.mult))
                s0, s1, s2 = (score[:, :, e] for e in range(NE))
                step(dve.tensor_tensor(gt[:, 0, :], s1, s0, ALU.is_gt))
                step(dve.tensor_tensor(gt[:, 1, :], s2, s0, ALU.is_gt))
                step(dve.tensor_tensor(gt[:, 2, :], s2, s1, ALU.is_gt))
                step(dve.tensor_scalar(ngt[:, :, :], gt[:, :, :], -1.0, 1.0, ALU.mult, ALU.add))
                step(dve.tensor_tensor(rank[:, 0, :], gt[:, 0, :], gt[:, 1, :], ALU.add))
                step(dve.tensor_tensor(rank[:, 1, :], ngt[:, 0, :], gt[:, 2, :], ALU.add))
                step(dve.tensor_tensor(rank[:, 2, :], ngt[:, 1, :], ngt[:, 2, :], ALU.add))
                step(dve.tensor_scalar(pick[:, 0, :, :], rank[:, :, :], 0.0, None, ALU.is_equal))
                step(dve.tensor_scalar(pick[:, 1, :, :], rank[:, :, :], 1.0, None, ALU.is_equal))
                assert steps[0] == R_PICK
                step(dve.tensor_tensor(top[:, 0, :], s0, s1, ALU.max))
                step(dve.tensor_tensor(top[:, 1, :], s0, s1, ALU.min))
                step(dve.tensor_tensor(top[:, 2, :], top[:, 0, :], s2, ALU.min))
                step(dve.tensor_tensor(topn[:, 0, :], top[:, 0, :], s2, ALU.max))
                step(dve.tensor_tensor(topn[:, 1, :], top[:, 1, :], top[:, 2, :], ALU.max))
                step(dve.tensor_tensor(top[:, 3, :], topn[:, 0, :], topn[:, 1, :], ALU.add))
                step(dve.tensor_scalar(top[:, 4, :], top[:, 3, :], 1e-8, None, ALU.add))
                step(dve.reciprocal(top[:, 5, :], top[:, 4, :]))
                step(dve.tensor_tensor(top[:, 6:8, :], topn[:, :, :], top[:, 5:6, :].to_broadcast((P, 2, NP)),
                                       ALU.mult))
                yield
                dve.wait_ge(picked_mm, k.i + 1)
                for i in range(2):
                    v = top[:, 6 + i:7 + i, :].to_broadcast((P, NE, NP))
                    w = slice(64 + i * NE * NP, 64 + (i + 1) * NE * NP)
                    step(dve.tensor_tensor(part[:, i, :, :],
                                           banks[:, YB[1], w].rearrange("p (e n) -> p e n", e=NE), v, ALU.mult))
                step(dve.tensor_tensor(coef[:, :, :], part[:, 0, :, :], part[:, 1, :, :], ALU.add))
                assert steps[0] == R_COEF
                flat = coef[:, :, :].rearrange("p e n -> p (e n)")
                dve.tensor_copy(coef_w.rearrange("p e n k -> p (e n) k"), wide(flat, P))\
                    .then_inc(coef_ready, 1)
                yield
                one = slice(0, 1)
                step(dve.tensor_copy(picked[one], banks[one, YB[1], 128:128 + 4 * NE * NP]
                                     .rearrange("p (h a n) -> p h a n", h=2, a=2)))
                step(dve.tensor_tensor(used[one].rearrange("p e n h -> p h (e n)"), picked[one, :, 0, :],
                                       picked[one, :, 1, :], ALU.add))
                both = used[one].rearrange("p e n h -> p e (n h)")
                for edge, col in ((first_in, C_FROM), (last_in, C_TO)):
                    row = cst[one, col:col + BB].rearrange("p (o b) -> p o b", o=1).to_broadcast((1, NE, BB))
                    step(dve.tensor_tensor(edge[one], both, row, ALU.mult))
                step(dve.tensor_reduce(s_from[one], first_in[one], AX.X, ALU.max))
                step(dve.tensor_reduce(s_to[one], last_in[one], AX.X, ALU.max))
                step(dve.tensor_tensor(s_sum[one], s_from[one], s_to[one], ALU.add))
                step(dve.tensor_scalar(s_size[one], s_sum[one], float(-BB), float(SPAN0), ALU.add, ALU.max))
                step(dve.tensor_tensor(s_end[one], s_from[one], s_size[one], ALU.max))
                step(dve.tensor_scalar(spans[:, 0, :], s_end[one], -1.0, float(BB), ALU.mult, ALU.add))
                step(dve.tensor_copy(spans[:, 1, :], s_size[one]))
                assert steps[0] == R_STEPS
                dve.sem_inc(spans_ready, 1)
                yield

            dve.sem_inc(w_lo, RING)
            for j in range(2):
                dve.sem_inc(drained[j], 1)

            def plain_slab(m, first):
                lo_piece(m * SLAB0 + 2, 2, 2)
                if not first:
                    softmax_sum(m - 1)
                rotate(0, m * SLAB0 + 1)
                rotated_lo(m, 0, m * 2 + 2)
                rotate(1, m * SLAB0 + 2)
                rotated_lo(m, 1, m + 2)
                if not first:
                    probs_lo(m - 1)
                lo_piece(m * SLAB0 + SLAB0, 0)
                if not first:
                    out_lo(m - 1, m - 1, YB)
                lo_piece(m * SLAB0 + (SLAB0 + 1), 1)
                values_lo(m)
                softmax_max(m)

            split_x(0)
            lo_piece(0, 0)
            lo_piece(1, 1)
            mixed_lo(0)
            dve.wait_ge(const_landed, 16 * N_CONST)
            dve.wait_ge(gwr_hi, 1)
            minus(gw_two[:, :, 4:4 + NE], gw[:, :, :], gw_two[:, :, 0:NE]).then_inc(gwr_lo, 1)
            plain_slab(0, True)
            with dve.Fori(1, NC) as m:
                plain_slab(m, False)
            softmax_sum(NC - 1)
            lo_piece(POS_O0 + 2, 2)
            probs_lo(NC - 1)
            out_lo(NC - 1, NC - 1, YB)

            def project_piece(pos, blk, n, ahead, batch, use):
                if n % HC == 0:
                    dve.wait_ge(xT_landed[n // HC], blk * 16 + 16)
                dve.wait_ge(gemm_done, pos + 1)
                dve.tensor_tensor(xT[:, n, :], banks[:, GB[n % 2], :], xT[:, n, :], ALU.add)\
                    .then_inc(drained[n % 2], 1)
                lo_piece(ahead, (n + 3) % RING)
                dve.wait_ge(x1_hi, batch + (n + 1))
                dve.wait_ge(drained[n % 2], use[n % 2] + (n // 2 + 2))
                minus(yy[:, n, :, 1, :], xT[:, n, :].rearrange("p (b t) -> p b t", b=BB),
                      yy[:, n, :, 0, :]).then_inc(x1_lo, 1)

            for n in range(NC):
                project_piece(POS_O0 + n, 0, n, POS_O0 + n + 3, 0, USE_SLABS)
                if n == 3:
                    split_x(1)

            def experts(k):
                def ahead(f, g=0):
                    off = k.f0 + f + 3
                    lo_piece(k.pos + (g * RING + off), off % RING)

                def scale(e, f, g=0):
                    if e * NC + f % NC > 1:
                        dve.wait_ge(act_lo, k.act + (g * RING + (e * NC + f % NC - 1)))
                    dve.wait_ge(drained[f % 2], k.use[f % 2] + (g * 2 + (k.fuse[f % 2] + f // 2 + 2)))
                    dve.tensor_tensor(scaled_t[:, f % 2, :], act_t[:, f % 2, :], banks[:, CB[e], :],
                                      ALU.mult).then_inc(act_scaled, 1)

                def scaled_lo(e, m, g=0):
                    count = k.act + (g * RING + (e * NC + m + 1))
                    dve.wait_ge(act_hi, count)
                    dve.wait_ge(act_scaled, count)
                    minus(ha_lo[:, g * RING + m, :], scaled_t[:, m % 2, :], ha_hi[:, g * RING + m, :])\
                        .then_inc(act_lo, 1)

                def share(e, f, g, span, split=True):
                    if split:
                        ahead(f, g)
                    m = g * RING + f % NC
                    dve.scalar_tensor_tensor(out=xT[:, m, :], in0=banks[:, CB[e], :],
                                             scalar=b2_t[:, e, bass.ds(m, 1)], in1=xT[:, m, :],
                                             op0=ALU.mult, op1=ALU.add).then_inc(bias_added, 1)
                    dve.wait_ge(gemm_done, k.pos + (g * RING + (k.f0 + f + 1)))
                    dve.wait_ge(bias_added, k.act + (g * RING + (e * NC + f % NC + 1)))
                    w = bass.ds(span[0] * T, span[1] * T)
                    dve.tensor_tensor(xT[:, m, w], banks[:, GB[f % 2], w], xT[:, m, w], ALU.add)\
                        .then_inc(drained[f % 2], 1)

                if k.last:
                    turned_y(k, BB - 1)
                else:
                    softmax_sum(k.slab + (NC - 1))
                chain = router(k)
                ahead(0)
                next(chain)
                if not k.last:
                    probs_lo(k.slab + (NC - 1))
                ahead(1)
                next(chain)
                if not k.last:
                    out_lo(k.slab + (NC - 1), NC - 1, SB)
                next(chain)
                ahead(2)
                next(chain)
                dve.wait_ge(coef_spread, k.i + 1)
                for m in range(2):
                    scale(0, m)
                for m in range(2):
                    scaled_lo(0, m)
                scale(0, 2)
                scaled_lo(0, 2)
                for m in range(3, NC):
                    scale(0, m)
                    ahead(m)
                    scaled_lo(0, m)
                    if m == 3:
                        dve.wait_ge(spans_ready, k.i + 1)
                for e in range(NE):
                    if e > 0:
                        with dve.Fori(0, NC // RING) as g:
                            for s in range(RING):
                                scale(e, e * 2 * NC + s, g)
                                ahead(e * 2 * NC + s, g)
                                scaled_lo(e, s, g)

                    def shares(first, n):
                        end = k.last and e == NE - 1
                        with dve.Fori(0, NC // RING - end) as g:
                            for s in range(RING):
                                share(e, (e * 2 + 1) * NC + s, g, (first, n))
                        if end:
                            for m in range(NC - RING, NC):
                                share(e, (e * 2 + 1) * NC + m, 0, (first, n), m < NC - 3)

                    for_span(dve, k, e, shares)

            def iteration(i, last):
                k = Counts(dve, i, last)

                def ahead(off):
                    lo_piece(k.pos + (off + 3), (off + 3) % RING)

                if last:
                    for b in range(BB):
                        for c in range(NC):
                            ahead(b * NC + c)
                            if c == 4 and b > 0:
                                turned_y(k, b - 1)
                    experts(k)
                    return
                mixed_lo(i + 1)
                for m in range(NC):
                    slab = k.slab + m
                    for w, piece in enumerate(order(m)):
                        off = m * NW + w
                        ahead(off)
                        if piece == "q":
                            if m > 0:
                                softmax_sum(slab - 1)
                            rotate(0, k.pos + (off + 1))
                            rotated_lo(slab, 0, k.use[0] + (2 * m + 2))
                        elif piece == "k":
                            rotate(1, k.pos + (off + 1))
                            rotated_lo(slab, 1, k.use[1] + (m + 2))
                            if m > 0:
                                probs_lo(slab - 1)
                        elif piece == "v" and m > 0:
                            out_lo(slab - 1, m - 1, SB)
                            if m == NC - 1:
                                turned_y(k, m)
                                values_lo(slab)
                        elif piece == 4 and m < NC - 1:
                            values_lo(slab)
                        elif piece == 6 and m > 0:
                            turned_y(k, m - 1)
                    softmax_max(slab)
                experts(k)
                for n in range(NC):
                    project_piece(k.pos + (POS_O + n), i + 1, n, k.pos + (POS_O + n + 3), k.slab,
                                  [k.use[j] + (USE_SLABS[j] + NF // 2) for j in range(2)])
                    if n == 3:
                        with dve.If(i < NBLK - 2):
                            split_x(i + 2)

            with dve.Fori(0, NBLK - 1) as i:
                iteration(i, False)
            iteration(NBLK - 1, True)


def kernel(**inputs):
    import concourse.bacc as _bacc
    from concourse.bass_utils import run_bass_kernel_spmd as _run

    a = {k: np.asarray(v) for k, v in inputs.items()}

    def pieces(w):
        return np.ascontiguousarray(w.reshape(NC, P, NC, P).transpose(2, 1, 0, 3)).reshape(NC, P, D)

    def even_odd(w):
        return w.reshape(D, HEADS, DH // 2, 2).transpose(0, 1, 3, 2).reshape(D, D)

    x = a["x"].reshape(B * T, D)
    arrays = {
        "x_pairs": np.ascontiguousarray(x.reshape(NBLK, NP, P, D).transpose(0, 2, 1, 3)),
        "x_cols": np.ascontiguousarray(x.reshape(NBLK, BT, NC, P).transpose(0, 3, 2, 1)),
        "ids_mix": a["itok_B_0_15"].reshape(1, B),
        "ids_adapter": a["itok_B_1_14"].reshape(1, B),
        "mix_w": a["L0_cond_weights"],
        "wq": pieces(even_odd(a["L0_attn_Wq"])),
        "wk": pieces(even_odd(a["L0_attn_Wk"])),
        "wv": pieces(a["L0_attn_Wv"]),
        "wo": pieces(a["L0_attn_Wo"]),
        "adapter_w": np.ascontiguousarray(a["L0_cond2_weight"].transpose(0, 2, 1)).reshape(-1, P, D),
        "gate_w": np.ascontiguousarray(a["L0_ffn_gate_w"][:D].reshape(NC, P, NE).transpose(1, 0, 2)),
        "gate_last": a["L0_ffn_gate_w"][D:D + 1],
        "gate_b": a["L0_ffn_gate_b"].reshape(1, NE),
        "w1": np.concatenate([pieces(w) for w in a["L0_ffn_w1"]]),
        "b1": np.ascontiguousarray(a["L0_ffn_b1"].reshape(NE, NC, P).transpose(2, 0, 1)),
        "w2": np.concatenate([pieces(w) for w in a["L0_ffn_w2"]]),
        "b2": np.ascontiguousarray(a["L0_ffn_b2"].reshape(NE, NC, P).transpose(2, 0, 1)),
        "consts": shape_constants(),
    }
    nc = _bacc.Bacc("TRN2", target_bir_lowering=False, num_devices=1)
    args = [nc.dram_tensor(f"in_{n}", v.shape, mybir.dt.from_np(v.dtype), kind="ExternalInput").ap()
            for n, v in arrays.items()]
    args.append(nc.dram_tensor("out_0", (NBLK, P, NC, BT), F32, kind="ExternalOutput").ap())
    build(nc, *args)
    r = _run(nc, [{f"in_{n}": v for n, v in arrays.items()}], core_ids=[0])
    got = r.results[0]["out_0"]
    return np.ascontiguousarray(got.transpose(0, 3, 2, 1)).reshape(B, T, D)
```

```python
from contextlib import ExitStack

import numpy as np

import concourse.bass as bass
from concourse import mybir

F32 = mybir.dt.float32
F32R = mybir.dt.float32r
I32 = mybir.dt.int32
ALU = mybir.AluOpType
ACT = mybir.ActivationFunctionType
AX = mybir.AxisListType

P = 128
B, T, D = 32, 64, 1024
HEADS, DH = 16, 64
NE = 3
BT = 512
BB = BT // T
NBLK = B * T // BT
NC = D // P
NP = BT // P
RING = 4
GC = 8
VISION = int(T * 0.3)


WARM = 13

WOVEN = ["q", 0, 1, "k", 2, 3, "v", 4, 5, 6, 7]
NW = len(WOVEN)
NWOVEN = 6
PLAIN = ["q", "k", "v"]
FIRST = BB - NWOVEN
WO = [("o", 0), ("o", 1)]
for _c in range(NC):
    WO += [(b, _c) for b in range(FIRST)] + ([("o", _c + 2)] if _c + 2 < NC else [])
NWO = len(WO)
X_PARTS = range(2, 7)
SLAB0 = RING
POS_O0 = NC * SLAB0
POS_IT = POS_O0 + NWO
NF = NE * 2 * NC
POS_F = NWOVEN * NW + (NC - NWOVEN) * len(PLAIN)
POS_FLAST = NWOVEN * NC
POS_O = POS_F + NF
POS_ALL = POS_O + NWO
FILLS0 = (NC + NWO // RING,) * 3 + (NWO // RING,)
FILLS = POS_ALL // RING
USE_SLABS = (2 * NC, NC)
USE0 = tuple(u + NC // 2 for u in USE_SLABS)
USE_IT = tuple(u + NF // 2 + NC // 2 for u in USE_SLABS)
R_SHIFT, R_PICK, R_COEF, R_STEPS = 9, 21, 33, 44
SPAN0 = 4

C_ID, C_TWO, C_SEL, C_MASK, C_ROT, C_ONE, C_EIGHT, C_FROM, C_TO = 0, 128, 192, 320, 448, 512, 516, 520, 528
C_END = C_TO + BB


def shape_constants():
    c = np.zeros((P, C_END), np.float32)
    tok = np.arange(P)
    same = tok[:, None] // T == tok[None, :] // T
    c[:, C_ID:C_ID + P] = np.eye(P)
    c[:, C_TWO:C_TWO + T] = tok[:, None] % T == np.arange(T)[None, :]
    c[:, C_SEL:C_SEL + P] = same & (tok[:, None] % T == 0)
    c[:, C_MASK:C_MASK + P] = np.where(same & (tok[None, :] <= tok[:, None]), 0.0, -1e30)
    freq = 1.0 / 10000.0 ** (np.arange(0, DH, 2) / DH)
    angle = freq[:, None] * np.arange(T)[None, :]
    plus, minus = np.cos(angle) + np.sin(angle), np.cos(angle) - np.sin(angle)
    c[:, C_ROT:C_ROT + T] = np.concatenate([plus, minus, plus, minus])
    c[:, C_ONE] = 1.0
    c[:, C_EIGHT:C_EIGHT + 4] = tok[:, None] % 4 == np.arange(4)[None, :]
    c[:, C_FROM:C_FROM + BB] = BB - np.arange(BB)
    c[:, C_TO:C_TO + BB] = 1 + np.arange(BB)
    return c


def order(m):
    return WOVEN if m < NWOVEN else PLAIN


def slab_pos(m):
    return min(m, NWOVEN) * NW + max(m - NWOVEN, 0) * len(PLAIN)


class Counts:

    def __init__(self, eng, i, last):
        fixed = isinstance(i, int)
        snap = (lambda v: v) if fixed else eng.snap
        self.i, self.last = i, last
        self.pos = snap(i * POS_ALL + POS_IT)
        self.fills = [snap(i * FILLS + FILLS0[s]) for s in (0, 3)]
        self.use = [snap(i * USE_IT[j] + USE0[j]) for j in range(2)]
        self.batch = snap(i * BB)
        self.slab = snap(i * NC + NC)
        self.act = snap(i * (NE * NC))
        self.f0 = POS_FLAST if last else POS_F
        self.fuse = (0, 0) if last else USE_SLABS

    def filled(self, off):
        return self.fills[off % RING == 3] + (off // RING + 1)


def build(nc, x_pairs, x_cols, ids_mix, ids_adapter, mix_w, wq, wk, wv, wo, adapter_w, gate_w,
          gate_last, gate_b, w1, b1, w2, b2, consts, out):
    ctx = ExitStack()
    with ctx:
        def sb(name, shape, dt=F32):
            return ctx.enter_context(nc.sbuf_tensor(name, shape, dt))

        def sem(name):
            return ctx.enter_context(nc.semaphore(name))

        raw = sb("raw", [P, RING, D])
        w_hi_t = sb("w_hi_t", [P, RING, D], F32R)
        w_lo_t = sb("w_lo_t", [P, RING, D], F32R)
        warm = raw[:, RING - 1, 0:BT]
        qk_land = sb("qk_land", [P, 2, NC, 2, 2, 32])
        ha_hi = sb("ha_hi", [P, NC, BT], F32R)
        ha_lo = sb("ha_lo", [P, NC, BT], F32R)
        ot_hi = sb("ot_hi", [P, NC, BT], F32R)
        ot_lo = sb("ot_lo", [P, NC, BT], F32R)
        yy = sb("yy", [P, NC, BB, 2, T], F32R)
        xT = sb("xT", [P, NC, BT])
        scratch = sb("scratch", [P, 4 * D])
        x_nat = scratch[:, :].rearrange("p (n d) -> p n d", n=NP)
        rot = scratch[:, 0:D].rearrange("p (j t) -> p j t", j=2)
        act_t = rot
        probs = scratch[:, D:2 * D].rearrange("p (h n k) -> p h n k", h=2, n=NP)
        scaled_t = scratch[:, D:2 * D].rearrange("p (j t) -> p j t", j=2)
        y_nat = scratch[:, 2 * D:3 * D]
        vT = scratch[:, 3 * D:3 * D + BT]
        spare = scratch[:, 3 * D + BT:4 * D]
        coef_w = scratch[:, 2 * D:2 * D + NE * NP * P].rearrange("p (e n k) -> p e n k", e=NE, n=NP)
        mix = qk_land[:, 1].rearrange("p c h u i -> p (c h u i)")[:, 0:NP * P].rearrange("p (n k) -> p n k", n=NP)
        qk_hi_t = sb("qk_hi_t", [P, 2, BT], F32R)
        qk_lo_t = sb("qk_lo_t", [P, 2, BT], F32R)
        v_hi_t = sb("v_hi_t", [P, NP, P], F32R)
        v_lo_t = sb("v_lo_t", [P, NP, P], F32R)
        mix_hi, mix_lo = v_hi_t, v_lo_t
        pt_hi_t = sb("pt_hi_t", [P, 2, BT], F32R)
        pt_lo_t = sb("pt_lo_t", [P, 2, BT], F32R)
        row_max = sb("row_max", [P, 2 * NP])
        row_sum = sb("row_sum", [P, 2 * NP])
        row_inv = sb("row_inv", [P, 2 * NP])
        junk = spare.rearrange("p (c t) -> p c t", c=NC)
        abs_sum_t = sb("abs_sum_t", [P, 2, BB])
        cst = sb("cst", [P, C_END])
        gw = sb("gw", [P, NC, NE])
        gw_two = sb("gw_two", [P, NC, GC], F32R)
        l_two = rot[0:8, 1, :]
        gw_last = sb("gw_last", [P, NE])
        gb = sb("gb", [P, NE])
        b1_t = sb("b1_t", [P, NE, NC])
        b2_t = sb("b2_t", [P, NE, NC])
        spans = sb("spans", [1, 2, NE], I32)
        idm = sb("idm", [1, B], I32)
        ida = sb("ida", [1, B], I32)
        taken = [0]

        def small(*dims):
            size = int(np.prod(dims))
            t = spare[:, taken[0]:taken[0] + size]
            taken[0] += size
            if len(dims) == 2:
                t = t.rearrange("p (a b) -> p a b", a=dims[0])
            if len(dims) == 3:
                t = t.rearrange("p (a b c) -> p a b c", a=dims[0], b=dims[1])
            return t

        vis_eps, vis_inv, ratio = small(BB), small(BB), small(NP)
        r_last, r_bias, logit, shifted, e_exp, score = (small(NP, NE) for _ in range(6))
        l_max, e_sum, e_inv = small(NP), small(NP), small(NP)
        gt, ngt, rank, pick = small(3, NP), small(3, NP), small(NE, NP), small(2, NE, NP)
        top, topn = small(8, NP), small(2, NP)
        part, coef = small(2, NE, NP), small(NE, NP)
        picked, used, first_in, last_in = small(2, 2, NE * NP), small(NE, NP, 2), small(NE, BB), small(NE, BB)
        s_from, s_to, s_sum, s_size, s_end = (small(NE) for _ in range(5))

        banks = ctx.enter_context(nc.psum_tensor("banks", [P, 8, 512], F32))
        GB = [0, 1]
        YB = [2, 3]
        TB = [4, 5]
        SB = [6, 7]
        MB = [TB[0]] + GB + [YB[1]]
        CB = [SB[0], SB[1], YB[0]]
        ident = cst[:, C_ID:C_ID + P]

        def o_banks(pair):
            return banks[:, pair[0]:pair[1] + 1, :].rearrange("p a (n h t) -> p (a n) h t", n=2, h=2)


        const_landed = sem("const_landed")
        ids_landed = sem("ids_landed")
        mix_zeroed = sem("mix_zeroed")
        warm_zeroed = sem("warm_zeroed")
        gw_zeroed = sem("gw_zeroed")
        raw_ready = [sem(f"raw_ready{s}") for s in range(RING)]
        qk_landed = [sem("q_landed"), sem("k_landed")]
        x_landed = [sem("x_landed0"), sem("x_landed1")]
        mix_landed = sem("mix_landed")
        xT_landed = [sem("xT_landed0"), sem("xT_landed1")]
        w_hi = sem("w_hi")
        w_lo = sem("w_lo")
        x_hi, x_lo = sem("x_hi"), sem("x_lo")
        mixw_hi, mixw_lo = sem("mixw_hi"), sem("mixw_lo")
        gwr_hi, gwr_lo = sem("gwr_hi"), sem("gwr_lo")
        mixed = sem("mixed")
        h_hi, h_lo = sem("h_hi"), sem("h_lo")
        gemm_done = sem("gemm_done")
        drained = [sem("drained0"), sem("drained1")]
        qk_hi, qk_lo = sem("qk_hi"), sem("qk_lo")
        vt_done, v_hi, v_lo = sem("vt_done"), sem("v_hi"), sem("v_lo")
        score_done = sem("score_done")
        sm_mask, sm_max, sm_shift = sem("sm_mask"), sem("sm_max"), sem("sm_shift")
        sm_exp, sm_sum, sm_inv, sm_probs = sem("sm_exp"), sem("sm_sum"), sem("sm_inv"), sem("sm_probs")
        pt_done, pt_hi, pt_lo = sem("pt_done"), sem("pt_hi"), sem("pt_lo")
        pv_done, o_hi, o_lo = sem("pv_done"), sem("o_hi"), sem("o_lo")
        x1_hi, x1_lo = sem("x1_hi"), sem("x1_lo")
        y_copied, abs_summed = sem("y_copied"), sem("abs_summed")
        yt_done, y_hi, y_lo = sem("yt_done"), sem("y_hi"), sem("y_lo")
        lt_done, lt_copied = sem("lt_done"), sem("lt_copied")
        router_mm, router_exp, picked_mm = sem("router_mm"), sem("router_exp"), sem("picked_mm")
        r_step = sem("r_step")
        coef_ready, coef_spread = sem("coef_ready"), sem("coef_spread")
        spans_ready = sem("spans_ready")
        act_scaled, act_hi, act_lo = sem("act_scaled"), sem("act_hi"), sem("act_lo")
        bias_added = sem("bias_added")
        out_stored = [sem("out_stored0"), sem("out_stored1")]

        block = ctx.enter_context(nc.Block())
        N_CONST = 7
        HC = NC // 2

        def out_banks(m):
            return YB if m >= NWOVEN else SB

        def adapter_banks(k, b):
            return ((YB, SB)[b % 2], 2) if k.last else (YB, 1)

        def for_span(eng, k, e, body):
            first = eng.value_load(spans[0:1, 0, bass.ds(e, 1)], min_val=0, max_val=BB - SPAN0)
            size = eng.value_load(spans[0:1, 1, bass.ds(e, 1)], min_val=SPAN0, max_val=BB)
            for n in range(SPAN0, BB + 1):
                with eng.If(size == n):
                    body(nc.s_assert_within(first, 0, BB - n, skip_runtime_bounds_check_because=
                                            "the router keeps first + size within the block"), n)

        @block.sync
        def _(sp):
            def fill(pos, s, src):
                sp.wait_ge(w_hi, pos + 1)
                sp.wait_ge(w_lo, pos + 1)
                sp.dma_start(raw[:, s, :], src).then_inc(raw_ready[s], 16)

            def land(m, js=(0, 1)):
                for j, w in [(j, (wq, wk)[j]) for j in js]:
                    sp.dma_start(qk_land[:, j], w[m, :, :]).then_inc(qk_landed[j], 16)

            def load_tokens(blk):
                for h in range(2):
                    p = slice(h * NP // 2, (h + 1) * NP // 2)
                    sp.dma_start(x_nat[:, p, :], x_pairs[blk, :, p, :]).then_inc(x_landed[h], 16)

            def load_mix(blk, zeroed):
                sp.wait_ge(mix_zeroed, zeroed)
                for b in range(BB):
                    a = sp.value_load(idm[0:1, bass.ds(blk * BB + b, 1)], min_val=0, max_val=15)
                    h = b % 2
                    sp.dma_start(mix[h * T:h * T + T, b // 2, h * T:h * T + T], mix_w[a, :, :])\
                      .then_inc(mix_landed, 16)

            def load_x(blk, zeroed):
                load_tokens(blk)
                load_mix(blk, zeroed)

            sp.dma_start(idm[:, :], ids_mix).then_inc(ids_landed, 16)
            load_tokens(0)
            land(0, (0,))
            sp.wait_ge(ids_landed, 16)
            load_mix(0, 1)
            sp.dma_start(ida[:, :], ids_adapter).then_inc(const_landed, 16)
            sp.dma_start(cst[:, :], consts).then_inc(const_landed, 16)
            sp.dma_start(gw[:, :, :], gate_w).then_inc(const_landed, 16)
            sp.dma_start(gw_last[:, :], gate_last.to_broadcast((P, NE))).then_inc(const_landed, 16)
            sp.dma_start(gb[:, :], gate_b.to_broadcast((P, NE))).then_inc(const_landed, 16)
            sp.dma_start(b1_t[:, :, :], b1).then_inc(const_landed, 16)
            sp.dma_start(b2_t[:, :, :], b2).then_inc(const_landed, 16)

            def land_again(m, j):
                sp.wait_ge(w_hi, m * SLAB0 + (j + 1))
                if j == 1:
                    sp.wait_ge(mixw_lo, 1)
                land(m, (j,))

            with sp.Fori(0, NC - 1) as m:
                land_again(m, 1)
                fill(m * SLAB0 + 2, 2, wv[m, :, :])
                land_again(m + 1, 0)
            land_again(NC - 1, 1)
            fill((NC - 1) * SLAB0 + 2, 2, wv[NC - 1, :, :])

            def fill_wo(pos0, js, blk):
                ids = [sp.value_load(ida[0:1, bass.ds(blk * BB + b, 1)], min_val=0, max_val=15)
                       for b in range(FIRST)]
                for j in js:
                    b, c = WO[j]
                    fill(pos0 + j, j % RING, wo[c, :, :] if b == "o" else adapter_w[ids[b] * NC + c, :, :])

            sp.wait_ge(const_landed, 16 * N_CONST)
            fill_wo(POS_O0, range(6), 0)
            sp.wait_ge(pt_done, 2 * NC)
            sp.wait_ge(vt_done, NC)
            load_x(1, 2)
            fill_wo(POS_O0, range(6, NWO), 0)

            def iteration(i, last):
                if not last:
                    mixw = sp.snap(i + 2)
                k = Counts(sp, i, last)
                if not last:
                    land(0, (0,))
                    sp.wait_ge(mixw_lo, mixw)
                    land(0, (1,))

                def adapters(b):
                    return sp.value_load(ida[0:1, bass.ds(i * BB + b, 1)], min_val=0, max_val=15) * NC

                if last:
                    firsts = [adapters(b) for b in range(FIRST, BB)]
                    for off in range(NWOVEN * NC):
                        fill(k.pos + off, off % RING, adapter_w[firsts[off // NC] + off % NC, :, :])
                else:
                    for m in range(NC):
                        a = adapters(m + FIRST) if m < NWOVEN else None
                        for w, piece in enumerate(order(m)):
                            off = slab_pos(m) + w
                            if piece == "v":
                                fill(k.pos + off, off % RING, wv[m, :, :])
                                if m < NC - 1:
                                    sp.wait_ge(w_hi, k.pos + (slab_pos(m) + order(m).index("k") + 1 + RING))
                                    land(m + 1)
                            elif isinstance(piece, int):
                                fill(k.pos + off, off % RING, adapter_w[a + piece, :, :])
                for e in range(NE):
                    for j, w in enumerate((w1, w2)):
                        with sp.Fori(0, NC // RING) as g:
                            for s in range(RING):
                                fill(k.pos + (g * RING + (k.f0 + (e * 2 + j) * NC + s)), s,
                                     w[g * RING + (e * NC + s), :, :])
                if not last:
                    with sp.If(i < NBLK - 2):
                        sp.wait_ge(act_lo, k.act + NE * NC)
                        blk = nc.s_assert_within(i + 2, 2, NBLK - 1, skip_runtime_bounds_check_because=
                                                 "the branch is taken only where i + 2 is a block")
                        load_x(blk, i + 3)
                    fill_wo(k.pos + POS_O, range(NWO), i + 1)

            with sp.Fori(0, NBLK - 1) as i:
                iteration(i, False)
            iteration(NBLK - 1, True)

        @block.gpsimd
        def _(pool):
            pool.memset(mix, 0.0).then_inc(mix_zeroed, 1)
            pool.memset(warm, 0.0).then_inc(warm_zeroed, 1)
            pool.memset(gw_two[:, :, :].bitcast(F32), 0.0).then_inc(gw_zeroed, 1)

            def take(j, slab, pos, s):
                r = raw[:, s, :].rearrange("p (c h u i) -> p c h u i", c=NC, h=2, u=2)
                even, odd = qk_land[:, j, :, :, 0, :], qk_land[:, j, :, :, 1, :]
                pool.wait_ge(qk_landed[j], slab * 16 + 16)
                pool.wait_ge(w_hi, pos + 1)
                pool.wait_ge(w_lo, pos + 1)
                pool.tensor_tensor(r[:, :, :, 0, :], even, odd, ALU.add)
                pool.tensor_tensor(r[:, :, :, 1, :], even, odd, ALU.subtract).then_inc(raw_ready[s], 16)

            def wide(t, k):
                return t.rearrange("p (n o) -> p n o", o=1).to_broadcast((P, t.shape[1], k))

            pr = probs.rearrange("p h n k -> p (h n) k")

            def softmax(slab):
                pool.wait_ge(sm_max, slab + 1)
                pool.tensor_tensor(pr, pr, wide(row_max[:, :], P), ALU.subtract).then_inc(sm_shift, 1)
                pool.wait_ge(sm_inv, slab + 1)
                pool.tensor_tensor(pr, pr, wide(row_inv[:, :], P), ALU.mult).then_inc(sm_probs, 1)

            def zero_mix():
                pool.memset(mix, 0.0).then_inc(mix_zeroed, 1)

            for j in range(2):
                take(j, 0, j, j)
            for h in range(2):
                c = slice(h * HC, h * HC + HC)
                pool.dma_start(xT[:, c, :], x_cols[0, :, c, :]).then_inc(xT_landed[h], 16)
            with pool.Fori(0, NC - 1) as m:
                for j in range(2):
                    take(j, m + 1, m * SLAB0 + (SLAB0 + j), j)
                softmax(m)
            softmax(NC - 1)
            zero_mix()

            def iteration(i, last):
                k = Counts(pool, i, last)
                if not last:
                    for m in range(NC):
                        for j, what in enumerate("qk"):
                            off = slab_pos(m) + order(m).index(what)
                            take(j, k.slab + m, k.pos + off, off % RING)
                        if m > 0:
                            softmax(k.slab + (m - 1))
                    softmax(k.slab + (NC - 1))
                    zero_mix()
                for n in range(NC):
                    use = k.fuse[n % 2] + NF // 2 - NC // 2 + n // 2
                    done = k.use[n % 2] + (use + 2)
                    if not last:
                        done = pool.snap(done)
                    pool.wait_ge(drained[n % 2], done)
                    pool.dma_start(out[i, :, n, :], xT[:, n, :]).then_inc(out_stored[n // HC], 16)
                    if not last and n in (HC, NC - 1):
                        h = int(n == NC - 1)
                        c = slice(h * HC, h * HC + HC)
                        pool.wait_ge(out_stored[h], i * (16 * HC) + 16 * HC)
                        pool.dma_start(xT[:, c, :], x_cols[i + 1, :, c, :]).then_inc(xT_landed[h], 16)

            with pool.Fori(0, NBLK - 1) as i:
                iteration(i, False)
            iteration(NBLK - 1, True)
            for h in range(2):
                pool.wait_ge(out_stored[h], 16 * HC * NBLK)

        @block.tensor
        def _(pe):
            def three(dst, l_hi, l_lo, r_hi, r_lo, start, stop):
                pe.matmul(dst, l_hi, r_hi, start=start, stop=False)
                pe.matmul(dst, l_hi, r_lo, start=False, stop=False)
                return pe.matmul(dst, l_lo, r_hi, start=False, stop=stop)

            def wait_piece(pos):
                pe.wait_ge(w_hi, pos + (1 + RING))
                pe.wait_ge(w_lo, pos + (1 + RING))

            def moving(src, c, span):
                first, n = span
                if src == "yy":
                    return yy[:, c, bass.ds(first, n), 0, :], yy[:, c, bass.ds(first, n), 1, :]
                hi, lo = {"ha": (ha_hi, ha_lo), "ot": (ot_hi, ot_lo)}[src]
                return hi[:, c, bass.ds(first * T, n * T)], lo[:, c, bass.ds(first * T, n * T)]

            def chunks(s, bank, src, cs, ready=None, span=(0, BB)):
                dst = banks[:, bank, bass.ds(span[0] * T, span[1] * T)]
                if src == "yy":
                    dst = dst.rearrange("p (b t) -> p b t", b=span[1])
                for c in cs:
                    if ready is not None:
                        ready_hi, ready_lo, base = ready
                        pe.wait_ge(ready_hi, base + (c + 1))
                        pe.wait_ge(ready_lo, base + (c + 1))
                    w = slice(c * P, c * P + P)
                    hi, lo = moving(src, c, span)
                    mm = three(dst, w_hi_t[:, s, w], w_lo_t[:, s, w], hi, lo, c == 0, c == NC - 1)
                return mm

            def gemm(pos, s, bank, use, src, ready=None, n=1, span=(0, BB)):
                wait_piece(pos)
                pe.wait_ge(drained[bank], use + 1)
                chunks(s, GB[bank], src, range(NC), ready, span).then_inc(gemm_done, n)

            def mix_tokens(blk, cs=range(NC)):
                pe.wait_ge(mixw_hi, blk + 1)
                pe.wait_ge(mixw_lo, blk + 1)
                pe.wait_ge(x_hi, blk * NP + NP)
                pe.wait_ge(x_lo, blk * NP + NP)
                for c in cs:
                    if c >= len(MB):
                        pe.wait_ge(h_hi, blk * NC + (c - 3))
                        pe.wait_ge(h_lo, blk * NC + (c - 3))
                    for p in range(NP):
                        w = slice(p * P, p * P + P)
                        mm = three(banks[:, MB[c % 4], w], ha_hi[:, c, w], ha_lo[:, c, w],
                                   mix_hi[:, p, :], mix_lo[:, p, :], True, True)
                    mm.then_inc(mixed, 1)

            def mix_left(base):
                pe.wait_ge(h_hi, base + 7)
                pe.wait_ge(h_lo, base + 7)

            def turn_probs(slab):
                pe.wait_ge(sm_probs, slab + 1)
                pe.wait_ge(v_hi, slab + 1)
                pe.wait_ge(v_lo, slab + 1)
                for h in range(2):
                    for p in range(NP):
                        mm = pe.transpose(banks[:, TB[h], p * P:p * P + P], probs[:, h, p, :], ident)
                    mm.then_inc(pt_done, 1)

            def outputs(slab, pair):
                pe.wait_ge(pt_hi, slab * 2 + 2)
                pe.wait_ge(pt_lo, slab * 2 + 2)
                for p in range(NP):
                    w = slice(p * P, p * P + P)
                    dst = banks[:, pair[p // 2], p % 2 * 2 * P:(p % 2 + 1) * 2 * P].rearrange("p (h t) -> p h t", h=2)
                    mm = three(dst, v_hi_t[:, p, :], v_lo_t[:, p, :], pt_hi_t[:, :, w], pt_lo_t[:, :, w],
                               True, True)
                mm.then_inc(pv_done, 1)

            def turn_values(copied):
                pe.wait_ge(drained[0], copied)
                for p in range(NP):
                    w = slice(p * P, p * P + P)
                    mm = pe.transpose(banks[:, TB[0], w], vT[:, w], ident)
                mm.then_inc(vt_done, 1)

            def scores(slab):
                pe.wait_ge(qk_hi, slab * 2 + 2)
                pe.wait_ge(qk_lo, slab * 2 + 2)
                for p in range(NP):
                    for h in range(2):
                        w, r = slice(p * P, p * P + P), slice(h * DH, h * DH + DH)
                        mm = three(banks[:, SB[h], w], qk_hi_t[r, 0, w], qk_lo_t[r, 0, w],
                                   qk_hi_t[r, 1, w], qk_lo_t[r, 1, w], True, True)
                mm.then_inc(score_done, 1)

            def adapter_piece(pos, s, batch, b, c, pair):
                wait_piece(pos)
                if b == 0:
                    pe.wait_ge(x1_hi, batch + (c + 1))
                    pe.wait_ge(x1_lo, batch + (c + 1))
                still = yy[:, c, b, :, :].rearrange("p u t -> p (u t)")
                for half in range(2):
                    w = slice(half * 512, half * 512 + 512)
                    pe.matmul(banks[:, pair[half], :], still, w_hi_t[:, s, w], start=(c == 0), stop=False)
                    mm = pe.matmul(banks[:, pair[half], :], still, w_lo_t[:, s, w],
                                   start=False, stop=(c == NC - 1))
                mm.then_inc(gemm_done, 1)

            def next_adapter(k, b, c, off):
                pair, lag = adapter_banks(k, b)
                if c == 0:
                    pe.wait_ge(y_copied, k.batch + (b - lag + 1))
                adapter_piece(k.pos + off, off % RING, k.batch, b, c, pair)

            def turn_y(k, b):
                pe.wait_ge(y_copied, k.batch + (b + 1))
                if b > 0:
                    wait_turned(k, b - 1)
                for c in range(NC):
                    mm = pe.matmul(banks[:, TB[1], c * T:c * T + T], y_nat[:, c * P:c * P + P],
                                   cst[:, C_TWO:C_TWO + T], start=True, stop=True)
                mm.then_inc(yt_done, 1)

            def wait_turned(k, b):
                pe.wait_ge(y_hi, k.batch + (b + 1))
                pe.wait_ge(y_lo, k.batch + (b + 1))
                pe.wait_ge(abs_summed, k.batch + (b + 1))

            def project(pos0, use, batch, js):
                for j in js:
                    b, c = WO[j]
                    if b == "o":
                        gemm(pos0 + j, j % RING, c % 2, use[c % 2] + c // 2, "ot")
                    else:
                        adapter_piece(pos0 + j, j % RING, batch, b, c, (YB, SB)[b])

            ones = cst[:, C_ONE:C_ONE + 1].to_broadcast((P, P))

            def plain_slab(m, first):
                pos = m * SLAB0
                if first:
                    mix_left(0)
                gemm(pos, 0, 0, m * 2, "ha", (h_hi, h_lo, 0) if first else None)
                gemm(pos + 1, 1, 1, m, "ha")
                if not first:
                    turn_probs(m - 1)
                gemm(pos + 2, 2, 0, m * 2 + 1, "ha", n=2)
                if not first:
                    outputs(m - 1, YB)
                turn_values(m * 2 + 3)
                scores(m)

            pe.wait_ge(warm_zeroed, 1)
            for _ in range(WARM):
                pe.matmul(banks[:, GB[0], :], warm[:, 0:P], warm, start=True, stop=True)
            mix_tokens(0)
            pe.wait_ge(const_landed, 16 * N_CONST)
            plain_slab(0, True)
            with pe.Fori(1, NC) as m:
                plain_slab(m, False)
            pe.wait_ge(gwr_hi, 1)
            pe.wait_ge(gwr_lo, 1)
            for n in range(2):
                wait_piece(POS_O0 + n)
                pe.wait_ge(drained[n], USE_SLABS[n] + 1)
                chunks(n, GB[n], "ot", range(NC - 1), (o_hi, o_lo, 0) if n == 0 else None)
            turn_probs(NC - 1)
            outputs(NC - 1, YB)
            for n in range(2):
                chunks(n, GB[n], "ot", [NC - 1], (o_hi, o_lo, 0)).then_inc(gemm_done, 1)
            project(POS_O0, USE_SLABS, 0, range(2, NWO - FIRST))
            mix_tokens(1, (0,))
            project(POS_O0, USE_SLABS, 0, range(NWO - FIRST, NWO))

            def woven_slab(k, m):
                slab = k.slab + m
                for w, piece in enumerate(order(m)):
                    off = slab_pos(m) + w
                    if piece == "q":
                        if m == 0:
                            mix_left(k.batch + NC)
                        gemm(k.pos + off, off % RING, 0, k.use[0] + 2 * m, "ha",
                             (h_hi, h_lo, k.batch + NC) if m == 0 else None)
                    elif piece == "k":
                        gemm(k.pos + off, off % RING, 1, k.use[1] + m, "ha")
                        if m > 0:
                            wait_turned(k, min(m, BB - 1))
                            turn_probs(slab - 1)
                    elif piece == "v":
                        gemm(k.pos + off, off % RING, 0, k.use[0] + (2 * m + 1), "ha")
                        if m == NWOVEN:
                            pe.wait_ge(y_copied, k.batch + BB)
                        if m > 0:
                            outputs(slab - 1, out_banks(m))
                        if m == NWOVEN:
                            turn_y(k, BB - 1)
                        if m >= NWOVEN:
                            turn_values(k.use[0] + (2 * m + 3))
                    else:
                        next_adapter(k, m + FIRST, piece, off)
                        if piece == 4:
                            turn_values(k.use[0] + (2 * m + 3))
                        if piece == 5 and m > 0:
                            turn_y(k, m + FIRST - 1)
                if 0 < m < NWOVEN:
                    pe.wait_ge(o_hi, slab)
                    pe.wait_ge(o_lo, slab)
                scores(slab)

            def expert_piece(k, f, g, ready=None, span=(0, BB)):
                src = "ha" if f // NC % 2 else "yy"
                gemm(k.pos + (g * RING + (k.f0 + f)), f % RING, f % 2,
                     k.use[f % 2] + (g * 2 + (k.fuse[f % 2] + f // 2)), src, ready, 1, span)

            def experts(k):
                if k.last:
                    turn_y(k, BB - 1)
                else:
                    pe.wait_ge(o_hi, k.slab + (NC - 1))
                    pe.wait_ge(o_lo, k.slab + (NC - 1))
                pe.wait_ge(y_hi, k.batch + BB)
                pe.wait_ge(y_lo, k.batch + BB)
                dst = banks[0:GC, YB[0], :].rearrange("p (b t) -> p b t", b=BB)
                for c in range(NC):
                    for u in range(2):
                        mm = pe.matmul(dst, gw_two[:, c, :], yy[:, c, :, u, :],
                                       start=(c == 0 and u == 0), stop=(c == NC - 1 and u == 1))
                mm.then_inc(lt_done, 1)
                expert_piece(k, 0, 0)
                pe.wait_ge(abs_summed, k.batch + BB)
                pe.matmul(banks[:, YB[1], 0:BB], ones, abs_sum_t[:, 0, :],
                          start=True, stop=True)
                pe.matmul(banks[:, YB[1], BB:2 * BB], ones, abs_sum_t[:, 1, :],
                          start=True, stop=True)
                pe.wait_ge(lt_copied, k.i + 1)
                for p in range(NP):
                    mm = pe.matmul(banks[:, YB[1], 32 + 4 * p:36 + 4 * p], l_two[:, p * P:p * P + P],
                                   cst[0:8, C_EIGHT:C_EIGHT + 4], start=True, stop=True)
                mm.then_inc(router_mm, 1)
                expert_piece(k, 1, 0)
                if not k.last:
                    wait_turned(k, BB - 1)
                    turn_probs(k.slab + (NC - 1))
                expert_piece(k, 2, 0)
                if not k.last:
                    outputs(k.slab + (NC - 1), SB)
                picks = pick[:, :, :, :].rearrange("p a e n -> p (a e n)")
                pe.wait_ge(r_step, k.i * R_STEPS + R_PICK)
                pe.matmul(banks[:, YB[1], 64:64 + 2 * NE * NP], cst[:, C_SEL:C_SEL + P],
                          picks, start=True, stop=True)
                for h in range(2):
                    w = slice(128 + h * 2 * NE * NP, 128 + (h + 1) * 2 * NE * NP)
                    mm = pe.matmul(banks[:, YB[1], w], cst[:, C_SEL + h * T:C_SEL + h * T + 1].to_broadcast((P, P)),
                                   picks, start=True, stop=True)
                mm.then_inc(picked_mm, 1)
                wait_piece(k.pos + (k.f0 + 3))
                pe.wait_ge(drained[1], k.use[1] + (k.fuse[1] + 2))
                chunks(3 % RING, GB[1], "yy", range(HC))
                pe.wait_ge(coef_ready, k.i + 1)
                if not k.last:
                    pe.wait_ge(o_hi, k.slab + NC)
                    pe.wait_ge(o_lo, k.slab + NC)
                for e in range(NE):
                    for p in range(NP):
                        mm = pe.matmul(banks[:, CB[e], p * P:p * P + P], coef_w[:, e, p, :],
                                       ident, start=True, stop=True)
                mm.then_inc(coef_spread, 1)
                chunks(3 % RING, GB[1], "yy", range(HC, NC)).then_inc(gemm_done, 1)
                pe.wait_ge(spans_ready, k.i + 1)
                for f in range(4, NC):
                    expert_piece(k, f, 0)
                for e in range(NE):
                    def pieces(first, n):
                        for j in range(int(e == 0), 2):
                            with pe.Fori(0, NC // RING) as g:
                                for s in range(RING):
                                    expert_piece(k, (e * 2 + j) * NC + s, g,
                                                 (act_hi, act_lo, k.act + e * NC) if s == 0 and j == 1 else None,
                                                 (first, n))

                    for_span(pe, k, e, pieces)

            def iteration(i, last):
                k = Counts(pe, i, last)
                if last:
                    turn_y(k, 0)
                    for b in range(FIRST, BB):
                        for c in range(NC):
                            next_adapter(k, b, c, (b - FIRST) * NC + c)
                            if c == 3:
                                turn_y(k, b - 1)
                    experts(k)
                    return
                mix_tokens(i + 1, (1, 2))
                pe.wait_ge(y_copied, k.batch + 1)
                mix_tokens(i + 1, (3,))
                turn_y(k, 0)
                mix_tokens(i + 1, (4, 5))
                turn_y(k, 1)
                mix_tokens(i + 1, (6, 7))
                for m in range(NC):
                    woven_slab(k, m)
                experts(k)
                use = [k.use[j] + (USE_SLABS[j] + NF // 2) for j in range(2)]
                project(k.pos + POS_O, use, k.slab, range(NWO - FIRST))
                with pe.If(i < NBLK - 2):
                    mix_tokens(i + 2, (0,))
                project(k.pos + POS_O, use, k.slab, range(NWO - FIRST, NWO))

            with pe.Fori(0, NBLK - 1) as i:
                iteration(i, False)
            iteration(NBLK - 1, True)

        @block.scalar
        def _(act):
            def copy(dst, src):
                return act.activation(dst, src, ACT.Copy)

            def split(pos, s, filled, n=1):
                act.wait_ge(raw_ready[s], filled * 16)
                if not (isinstance(pos, int) and pos < RING):
                    act.wait_ge(gemm_done, pos - (RING - 1))
                copy(w_hi_t[:, s, :], raw[:, s, :]).then_inc(w_hi, n)

            def split_x(blk, parts=range(NP + 1)):
                for p in parts:
                    if p < NP:
                        act.wait_ge(x_landed[p // (NP // 2)], blk * 16 + 16)
                        copy(ha_hi[:, :, p * P:p * P + P], x_nat[:, p, :].rearrange("p (c d) -> p c d", c=NC))\
                            .then_inc(x_hi, 1)
                    else:
                        act.wait_ge(mix_landed, blk * (16 * BB) + 16 * BB)
                        copy(mix_hi[:, :, :], mix).then_inc(mixw_hi, 1)

            def mixed_hi(blk, cs=range(NC)):
                for c in cs:
                    act.wait_ge(mixed, blk * NC + (c + 1))
                    copy(ha_hi[:, c, :], banks[:, MB[c % 4], :]).then_inc(h_hi, 1)

            def rotated_hi(slab, j, rotated):
                act.wait_ge(drained[j], rotated)
                copy(qk_hi_t[:, j, :], rot[:, j, :]).then_inc(qk_hi, 1)

            def exp(slab):
                act.wait_ge(sm_shift, slab + 1)
                act.activation(probs, probs, ACT.Exp).then_inc(sm_exp, 1)

            def probs_hi(slab):
                for h in range(2):
                    act.wait_ge(pt_done, slab * 2 + (h + 1))
                    copy(pt_hi_t[:, h, :], banks[:, TB[h], :]).then_inc(pt_hi, 1)

            def copy_values(done):
                act.wait_ge(gemm_done, done)
                copy(vT, banks[:, GB[0], :]).then_inc(drained[0], 1)

            def values_hi(slab):
                act.wait_ge(vt_done, slab + 1)
                copy(v_hi_t[:, :, :].rearrange("p n k -> p (n k)"), banks[:, TB[0], :]).then_inc(v_hi, 1)

            def out_hi(slab, m, pair):
                act.wait_ge(pv_done, slab + 1)
                for h in range(2):
                    r = slice(h * DH, h * DH + DH)
                    ins = copy(ot_hi[r, m, :].rearrange("p (n t) -> p n t", n=NP), o_banks(pair)[r, :, h, :])
                ins.then_inc(o_hi, 1)

            def x1_piece(batch, n, added):
                act.wait_ge(drained[n % 2], added)
                copy(yy[:, n, :, 0, :], xT[:, n, :].rearrange("p (b t) -> p b t", b=BB)).then_inc(x1_hi, 1)

            def copy_y(b, done, pair):
                act.wait_ge(gemm_done, done)
                copy(y_nat, banks[:, pair[0]:pair[0] + 2, :].rearrange("p a n -> p (a n)")).then_inc(y_copied, 1)

            def turned_y(k, b):
                act.wait_ge(yt_done, k.batch + (b + 1))
                yt = banks[:, TB[1], :].rearrange("p (c t) -> p c t", c=NC)
                copy(yy[:, :, b, 0, :], yt).then_inc(y_hi, 1)
                for u, t in enumerate((slice(VISION, T), slice(0, VISION))):
                    ins = act.activation(junk[:, :, t], yt[:, :, t], ACT.Abs, accum_out=abs_sum_t[:, u, b:b + 1])
                ins.then_inc(abs_summed, 1)

            act.sem_inc(w_hi, RING)

            def plain_slab(m, first):
                split(m * SLAB0 + 2, 2, m + 1, 2)
                if not first:
                    exp(m - 1)
                rotated_hi(m, 0, m * 2 + 2)
                rotated_hi(m, 1, m + 2)
                if not first:
                    probs_hi(m - 1)
                split(m * SLAB0 + SLAB0, 0, m + 2)
                copy_values(m * SLAB0 + 4)
                if not first:
                    out_hi(m - 1, m - 1, YB)
                split(m * SLAB0 + (SLAB0 + 1), 1, m + 2)
                values_hi(m)

            split_x(0)
            mixed_hi(0, range(NC - 3))
            split(0, 0, 1)
            mixed_hi(0, range(NC - 3, NC))
            split(1, 1, 1)
            act.wait_ge(const_landed, 16 * N_CONST)
            act.wait_ge(gw_zeroed, 1)
            copy(gw_two[:, :, 0:NE], gw[:, :, :]).then_inc(gwr_hi, 1)
            plain_slab(0, True)
            with act.Fori(1, NC) as m:
                plain_slab(m, False)
            exp(NC - 1)
            k0 = Counts(act, 0, False)
            split(POS_O0 + 2, 2, k0.filled(2 - NWO))
            probs_hi(NC - 1)
            out_hi(NC - 1, NC - 1, YB)

            def project(k, off0, batch, use, split_next):
                for j, (b, n) in enumerate(WO):
                    if j == NWO - 1:
                        copy_y(0, k.pos + (off0 + j), YB)
                    split(k.pos + (off0 + j + 3), (j + 3) % RING, k.filled(off0 + j + 3))
                    if b == "o":
                        x1_piece(batch, n, use[n % 2] + (n // 2 + 2))
                        if n in X_PARTS:
                            split_next(X_PARTS.index(n))

            project(k0, -NWO, 0, USE_SLABS, lambda part: split_x(1, [part]))

            def experts(k):
                def split_ahead(f, g=0):
                    off = k.f0 + f + 3
                    split(k.pos + (g * RING + off), off % RING, k.filled(off) + g)

                def activate(e, f, g, func):
                    act.wait_ge(gemm_done, k.pos + (g * RING + (k.f0 + f + 1)))
                    act.activation(act_t[:, f % 2, :], banks[:, GB[f % 2], :], func,
                                   bias=b1_t[:, e, bass.ds(g * RING + f % NC, 1)])\
                        .then_inc(drained[f % 2], 1)

                def scaled_hi(e, m, g):
                    act.wait_ge(act_scaled, k.act + (g * RING + (e * NC + m + 1)))
                    copy(ha_hi[:, g * RING + m, :], scaled_t[:, m % 2, :]).then_inc(act_hi, 1)

                if k.last:
                    copy_y(BB - 1, k.pos + k.f0, SB)
                    turned_y(k, BB - 1)
                else:
                    exp(k.slab + (NC - 1))
                act.wait_ge(lt_done, k.i + 1)
                copy(l_two[:, :], banks[0:8, YB[0], :]).then_inc(lt_copied, 1)
                split_ahead(0)
                activate(0, 0, 0, ACT.Tanh)
                act.wait_ge(r_step, k.i * R_STEPS + R_SHIFT)
                act.activation(e_exp[:, :, :], shifted[:, :, :], ACT.Exp).then_inc(router_exp, 1)
                split_ahead(1)
                activate(0, 1, 0, ACT.Tanh)
                if not k.last:
                    probs_hi(k.slab + (NC - 1))
                split_ahead(2)
                if not k.last:
                    out_hi(k.slab + (NC - 1), NC - 1, SB)
                scaled_hi(0, 0, 0)
                activate(0, 2, 0, ACT.Tanh)
                scaled_hi(0, 1, 0)
                scaled_hi(0, 2, 0)
                for m in range(3, NC):
                    split_ahead(m)
                    activate(0, m, 0, ACT.Tanh)
                    scaled_hi(0, m, 0)
                for e, func in enumerate((ACT.Tanh, ACT.Gelu, ACT.Silu)):
                    if e > 0:
                        with act.Fori(0, NC // RING) as g:
                            for s in range(RING):
                                split_ahead(e * 2 * NC + s, g)
                                activate(e, e * 2 * NC + s, g, func)
                                scaled_hi(e, s, g)
                    if e < NE - 1 or not k.last:
                        with act.Fori(0, NC // RING) as g:
                            for s in range(RING):
                                split_ahead((e * 2 + 1) * NC + s, g)
                    else:
                        for m in range(NC - 3):
                            split_ahead((e * 2 + 1) * NC + m)

            def iteration(i, last):
                k = Counts(act, i, last)

                def ahead(off):
                    split(k.pos + (off + 3), (off + 3) % RING, k.filled(off + 3))

                if last:
                    turned_y(k, 0)
                    copy_y(1, k.pos, SB)
                    for b in range(FIRST, BB):
                        for c in range(NC):
                            off = (b - FIRST) * NC + c
                            if c == 0 and b > FIRST:
                                copy_y(b - 1, k.pos + off, adapter_banks(k, b - 1)[0])
                            ahead(off)
                            if c == 4:
                                turned_y(k, b - 1)
                    experts(k)
                    return
                mixed_hi(i + 1, range(4))
                turned_y(k, 0)
                copy_y(1, k.pos, SB)
                mixed_hi(i + 1, (4, 5))
                turned_y(k, 1)
                mixed_hi(i + 1, (6, 7))
                for m in range(NC):
                    slab = k.slab + m
                    if m >= NWOVEN:
                        off = slab_pos(m)
                        if m == NWOVEN:
                            copy_y(BB - 1, k.pos + off, YB)
                        exp(slab - 1)
                        rotated_hi(slab, 0, k.use[0] + (2 * m + 2))
                        rotated_hi(slab, 1, k.use[1] + (m + 2))
                        probs_hi(slab - 1)
                        ahead(off)
                        copy_values(k.pos + (off + 3))
                        out_hi(slab - 1, m - 1, out_banks(m))
                        if m == NWOVEN:
                            turned_y(k, BB - 1)
                        ahead(off + 1)
                        values_hi(slab)
                        ahead(off + 2)
                        continue
                    for w, piece in enumerate(order(m)):
                        off = slab_pos(m) + w
                        if piece == "q":
                            if m > 0:
                                copy_y(m + FIRST - 1, k.pos + off, YB)
                            ahead(off)
                            if m > 0:
                                exp(slab - 1)
                            rotated_hi(slab, 0, k.use[0] + (2 * m + 2))
                        elif piece == "k":
                            ahead(off)
                            rotated_hi(slab, 1, k.use[1] + (m + 2))
                            if m > 0:
                                probs_hi(slab - 1)
                        elif piece == "v":
                            ahead(off)
                            copy_values(k.pos + (off + 1))
                            if m > 0:
                                out_hi(slab - 1, m - 1, out_banks(m))
                        else:
                            ahead(off)
                            if piece == 4:
                                values_hi(slab)
                            if piece == 6 and m > 0:
                                turned_y(k, m + FIRST - 1)
                experts(k)

                def split_next(part):
                    with act.If(i < NBLK - 2):
                        split_x(i + 2, [part])

                project(k, POS_O, k.slab, [k.use[j] + (USE_SLABS[j] + NF // 2) for j in range(2)], split_next)

            with act.Fori(0, NBLK - 1) as i:
                iteration(i, False)
            iteration(NBLK - 1, True)

        @block.vector
        def _(dve):
            def minus(dst, src, hi):
                return dve.tensor_tensor(dst, src, hi.bitcast(F32), ALU.subtract)

            def lo_piece(pos, s, n=1):
                dve.wait_ge(w_hi, pos + (1 + RING))
                minus(w_lo_t[:, s, :], raw[:, s, :], w_hi_t[:, s, :]).then_inc(w_lo, n)

            rot_f = cst[:, C_ROT:C_ROT + T].rearrange("p (o t) -> p o t", o=1).to_broadcast((P, BB, T))
            mask = cst[:, C_MASK:C_MASK + P].rearrange("p (o t) -> p o t", o=1).to_broadcast((P, NP, P))

            def wide(t, k):
                return t.rearrange("p (n o) -> p n o", o=1).to_broadcast((P, t.shape[1], k))

            def split_x(blk, parts=range(NP + 1)):
                for p in parts:
                    w = slice(p * P, p * P + P)
                    if p < NP:
                        dve.wait_ge(x_hi, blk * NP + (p + 1))
                        minus(ha_lo[:, :, w], x_nat[:, p, :].rearrange("p (c d) -> p c d", c=NC),
                              ha_hi[:, :, w]).then_inc(x_lo, 1)
                    else:
                        dve.wait_ge(mixw_hi, blk + 1)
                        minus(mix_lo[:, :, :], mix, mix_hi[:, :, :]).then_inc(mixw_lo, 1)

            def mixed_lo(blk, cs=range(NC)):
                for c in cs:
                    dve.wait_ge(h_hi, blk * NC + (c + 1))
                    minus(ha_lo[:, c, :], banks[:, MB[c % 4], :], ha_hi[:, c, :]).then_inc(h_lo, 1)

            def rotate(j, done):
                dve.wait_ge(gemm_done, done)
                dve.tensor_tensor(rot[:, j, :].rearrange("p (b t) -> p b t", b=BB),
                                  banks[:, GB[j], :].rearrange("p (b t) -> p b t", b=BB), rot_f, ALU.mult)\
                    .then_inc(drained[j], 1)

            def rotated_lo(slab, j, rotated):
                dve.wait_ge(qk_hi, slab * 2 + (j + 1))
                dve.wait_ge(drained[j], rotated)
                minus(qk_lo_t[:, j, :], rot[:, j, :], qk_hi_t[:, j, :]).then_inc(qk_lo, 1)

            pr = probs.rearrange("p h n k -> p (h n) k")

            def softmax_max(slab):
                dve.wait_ge(score_done, slab + 1)
                for h in range(2):
                    dve.scalar_tensor_tensor(
                        out=probs[:, h, :, :], in0=banks[:, SB[h], :].rearrange("p (n k) -> p n k", n=NP),
                        scalar=0.5 / DH ** 0.5, in1=mask, op0=ALU.mult, op1=ALU.add).then_inc(sm_mask, 1)
                dve.wait_ge(sm_mask, slab * 2 + 2)
                dve.tensor_reduce(row_max[:, :], pr, AX.X, ALU.max).then_inc(sm_max, 1)

            def softmax_sum(slab):
                dve.wait_ge(sm_exp, slab + 1)
                dve.tensor_reduce(row_sum[:, :], pr, AX.X, ALU.add).then_inc(sm_sum, 1)
                dve.wait_ge(sm_sum, slab + 1)
                dve.reciprocal(row_inv[:, :], row_sum[:, :]).then_inc(sm_inv, 1)

            def probs_lo(slab):
                for h in range(2):
                    dve.wait_ge(pt_hi, slab * 2 + (h + 1))
                    minus(pt_lo_t[:, h, :], banks[:, TB[h], :], pt_hi_t[:, h, :]).then_inc(pt_lo, 1)

            def values_lo(slab):
                dve.wait_ge(v_hi, slab + 1)
                minus(v_lo_t[:, :, :].rearrange("p n k -> p (n k)"), banks[:, TB[0], :],
                      v_hi_t[:, :, :].rearrange("p n k -> p (n k)")).then_inc(v_lo, 1)

            def out_lo(slab, m, pair):
                dve.wait_ge(o_hi, slab + 1)
                for h in range(2):
                    r = slice(h * DH, h * DH + DH)
                    ins = minus(ot_lo[r, m, :].rearrange("p (n t) -> p n t", n=NP), o_banks(pair)[r, :, h, :],
                                ot_hi[r, m, :].rearrange("p (n t) -> p n t", n=NP))
                ins.then_inc(o_lo, 1)

            def turned_y(k, b):
                dve.wait_ge(y_hi, k.batch + (b + 1))
                dve.wait_ge(abs_summed, k.batch + (b + 1))
                minus(yy[:, :, b, 1, :], banks[:, TB[1], :].rearrange("p (c t) -> p c t", c=NC),
                      yy[:, :, b, 0, :]).then_inc(y_lo, 1)

            def router(k):
                base = k.i * R_STEPS if isinstance(k.i, int) else dve.snap(k.i * R_STEPS)
                steps = [0]

                def step(ins):
                    ins.then_inc(r_step, 1)
                    steps[0] += 1
                    dve.wait_ge(r_step, base + steps[0])

                dve.wait_ge(router_mm, k.i + 1)
                step(dve.tensor_scalar(vis_eps[:, :], banks[:, YB[1], BB:2 * BB], 1.0 / (VISION * D), 1e-8,
                                       ALU.mult, ALU.add))
                step(dve.reciprocal(vis_inv[:, :], vis_eps[:, :]))
                for h in range(2):
                    r = slice(h * T, h * T + T)
                    step(dve.scalar_tensor_tensor(out=ratio[r, :], in0=banks[r, YB[1], h:BB:2],
                                                  scalar=1.0 / ((T - VISION) * D), in1=vis_inv[r, h:BB:2],
                                                  op0=ALU.mult, op1=ALU.mult))
                last = gw_last[:, :].rearrange("p (o e) -> p o e", o=1).to_broadcast((P, NP, NE))
                bias = gb[:, :].rearrange("p (o e) -> p o e", o=1).to_broadcast((P, NP, NE))
                rows = banks[:, YB[1], 32:32 + 4 * NP].rearrange("p (n e) -> p n e", n=NP)[:, :, 0:NE]
                step(dve.tensor_tensor(r_last[:, :, :], wide(ratio[:, :], NE), last, ALU.mult))
                step(dve.tensor_tensor(r_bias[:, :, :], r_last[:, :, :], rows, ALU.add))
                step(dve.tensor_tensor(logit[:, :, :], r_bias[:, :, :], bias, ALU.add))
                step(dve.tensor_reduce(l_max[:, :], logit[:, :, :], AX.X, ALU.max))
                step(dve.tensor_tensor(shifted[:, :, :], logit[:, :, :], wide(l_max[:, :], NE), ALU.subtract))
                assert steps[0] == R_SHIFT
                yield
                dve.wait_ge(router_exp, k.i + 1)
                step(dve.tensor_reduce(e_sum[:, :], e_exp[:, :, :], AX.X, ALU.add))
                step(dve.reciprocal(e_inv[:, :], e_sum[:, :]))
                step(dve.tensor_tensor(score[:, :, :], e_exp[:, :, :], wide(e_inv[:, :], NE), ALU.mult))
                s0, s1, s2 = (score[:, :, e] for e in range(NE))
                step(dve.tensor_tensor(gt[:, 0, :], s1, s0, ALU.is_gt))
                step(dve.tensor_tensor(gt[:, 1, :], s2, s0, ALU.is_gt))
                step(dve.tensor_tensor(gt[:, 2, :], s2, s1, ALU.is_gt))
                step(dve.tensor_scalar(ngt[:, :, :], gt[:, :, :], -1.0, 1.0, ALU.mult, ALU.add))
                step(dve.tensor_tensor(rank[:, 0, :], gt[:, 0, :], gt[:, 1, :], ALU.add))
                step(dve.tensor_tensor(rank[:, 1, :], ngt[:, 0, :], gt[:, 2, :], ALU.add))
                step(dve.tensor_tensor(rank[:, 2, :], ngt[:, 1, :], ngt[:, 2, :], ALU.add))
                step(dve.tensor_scalar(pick[:, 0, :, :], rank[:, :, :], 0.0, None, ALU.is_equal))
                step(dve.tensor_scalar(pick[:, 1, :, :], rank[:, :, :], 1.0, None, ALU.is_equal))
                assert steps[0] == R_PICK
                step(dve.tensor_tensor(top[:, 0, :], s0, s1, ALU.max))
                step(dve.tensor_tensor(top[:, 1, :], s0, s1, ALU.min))
                step(dve.tensor_tensor(top[:, 2, :], top[:, 0, :], s2, ALU.min))
                step(dve.tensor_tensor(topn[:, 0, :], top[:, 0, :], s2, ALU.max))
                step(dve.tensor_tensor(topn[:, 1, :], top[:, 1, :], top[:, 2, :], ALU.max))
                step(dve.tensor_tensor(top[:, 3, :], topn[:, 0, :], topn[:, 1, :], ALU.add))
                step(dve.tensor_scalar(top[:, 4, :], top[:, 3, :], 1e-8, None, ALU.add))
                step(dve.reciprocal(top[:, 5, :], top[:, 4, :]))
                step(dve.tensor_tensor(top[:, 6:8, :], topn[:, :, :], top[:, 5:6, :].to_broadcast((P, 2, NP)),
                                       ALU.mult))
                yield
                dve.wait_ge(picked_mm, k.i + 1)
                for i in range(2):
                    v = top[:, 6 + i:7 + i, :].to_broadcast((P, NE, NP))
                    w = slice(64 + i * NE * NP, 64 + (i + 1) * NE * NP)
                    step(dve.tensor_tensor(part[:, i, :, :],
                                           banks[:, YB[1], w].rearrange("p (e n) -> p e n", e=NE), v, ALU.mult))
                step(dve.tensor_tensor(coef[:, :, :], part[:, 0, :, :], part[:, 1, :, :], ALU.add))
                assert steps[0] == R_COEF
                flat = coef[:, :, :].rearrange("p e n -> p (e n)")
                dve.tensor_copy(coef_w.rearrange("p e n k -> p (e n) k"), wide(flat, P))\
                    .then_inc(coef_ready, 1)
                yield
                one = slice(0, 1)
                step(dve.tensor_copy(picked[one], banks[one, YB[1], 128:128 + 4 * NE * NP]
                                     .rearrange("p (h a n) -> p h a n", h=2, a=2)))
                step(dve.tensor_tensor(used[one].rearrange("p e n h -> p h (e n)"), picked[one, :, 0, :],
                                       picked[one, :, 1, :], ALU.add))
                both = used[one].rearrange("p e n h -> p e (n h)")
                for edge, col in ((first_in, C_FROM), (last_in, C_TO)):
                    row = cst[one, col:col + BB].rearrange("p (o b) -> p o b", o=1).to_broadcast((1, NE, BB))
                    step(dve.tensor_tensor(edge[one], both, row, ALU.mult))
                step(dve.tensor_reduce(s_from[one], first_in[one], AX.X, ALU.max))
                step(dve.tensor_reduce(s_to[one], last_in[one], AX.X, ALU.max))
                step(dve.tensor_tensor(s_sum[one], s_from[one], s_to[one], ALU.add))
                step(dve.tensor_scalar(s_size[one], s_sum[one], float(-BB), float(SPAN0), ALU.add, ALU.max))
                step(dve.tensor_tensor(s_end[one], s_from[one], s_size[one], ALU.max))
                step(dve.tensor_scalar(spans[:, 0, :], s_end[one], -1.0, float(BB), ALU.mult, ALU.add))
                step(dve.tensor_copy(spans[:, 1, :], s_size[one]))
                assert steps[0] == R_STEPS
                dve.sem_inc(spans_ready, 1)
                yield

            dve.sem_inc(w_lo, RING)
            for j in range(2):
                dve.sem_inc(drained[j], 1)

            def plain_slab(m, first):
                lo_piece(m * SLAB0 + 2, 2, 2)
                if not first:
                    softmax_sum(m - 1)
                rotate(0, m * SLAB0 + 1)
                rotated_lo(m, 0, m * 2 + 2)
                rotate(1, m * SLAB0 + 2)
                rotated_lo(m, 1, m + 2)
                if not first:
                    probs_lo(m - 1)
                lo_piece(m * SLAB0 + SLAB0, 0)
                if not first:
                    out_lo(m - 1, m - 1, YB)
                lo_piece(m * SLAB0 + (SLAB0 + 1), 1)
                values_lo(m)
                softmax_max(m)

            split_x(0)
            mixed_lo(0, range(NC - 3))
            lo_piece(0, 0)
            mixed_lo(0, range(NC - 3, NC))
            lo_piece(1, 1)
            dve.wait_ge(const_landed, 16 * N_CONST)
            dve.wait_ge(gwr_hi, 1)
            minus(gw_two[:, :, 4:4 + NE], gw[:, :, :], gw_two[:, :, 0:NE]).then_inc(gwr_lo, 1)
            plain_slab(0, True)
            with dve.Fori(1, NC) as m:
                plain_slab(m, False)
            softmax_sum(NC - 1)
            lo_piece(POS_O0 + 2, 2)
            probs_lo(NC - 1)
            out_lo(NC - 1, NC - 1, YB)

            def project(pos0, blk, batch, use, split_next):
                for j, (b, n) in enumerate(WO):
                    lo_piece(pos0 + j + 3, (j + 3) % RING)
                    if b != "o":
                        continue
                    if n % HC == 0:
                        dve.wait_ge(xT_landed[n // HC], blk * 16 + 16)
                    dve.wait_ge(gemm_done, pos0 + j + 1)
                    dve.tensor_tensor(xT[:, n, :], banks[:, GB[n % 2], :], xT[:, n, :], ALU.add)\
                        .then_inc(drained[n % 2], 1)
                    dve.wait_ge(x1_hi, batch + (n + 1))
                    dve.wait_ge(drained[n % 2], use[n % 2] + (n // 2 + 2))
                    minus(yy[:, n, :, 1, :], xT[:, n, :].rearrange("p (b t) -> p b t", b=BB),
                          yy[:, n, :, 0, :]).then_inc(x1_lo, 1)
                    if n in X_PARTS:
                        split_next(X_PARTS.index(n))

            project(POS_O0, 0, 0, USE_SLABS, lambda part: split_x(1, [part]))

            def experts(k):
                def ahead(f, g=0):
                    off = k.f0 + f + 3
                    lo_piece(k.pos + (g * RING + off), off % RING)

                def scale(e, f, g=0):
                    if e * NC + f % NC > 1:
                        dve.wait_ge(act_lo, k.act + (g * RING + (e * NC + f % NC - 1)))
                    dve.wait_ge(drained[f % 2], k.use[f % 2] + (g * 2 + (k.fuse[f % 2] + f // 2 + 2)))
                    dve.tensor_tensor(scaled_t[:, f % 2, :], act_t[:, f % 2, :], banks[:, CB[e], :],
                                      ALU.mult).then_inc(act_scaled, 1)

                def scaled_lo(e, m, g=0):
                    count = k.act + (g * RING + (e * NC + m + 1))
                    dve.wait_ge(act_hi, count)
                    dve.wait_ge(act_scaled, count)
                    minus(ha_lo[:, g * RING + m, :], scaled_t[:, m % 2, :], ha_hi[:, g * RING + m, :])\
                        .then_inc(act_lo, 1)

                def share(e, f, g, span, split=True):
                    if split:
                        ahead(f, g)
                    m = g * RING + f % NC
                    dve.scalar_tensor_tensor(out=xT[:, m, :], in0=banks[:, CB[e], :],
                                             scalar=b2_t[:, e, bass.ds(m, 1)], in1=xT[:, m, :],
                                             op0=ALU.mult, op1=ALU.add).then_inc(bias_added, 1)
                    dve.wait_ge(gemm_done, k.pos + (g * RING + (k.f0 + f + 1)))
                    dve.wait_ge(bias_added, k.act + (g * RING + (e * NC + f % NC + 1)))
                    w = bass.ds(span[0] * T, span[1] * T)
                    dve.tensor_tensor(xT[:, m, w], banks[:, GB[f % 2], w], xT[:, m, w], ALU.add)\
                        .then_inc(drained[f % 2], 1)

                if k.last:
                    turned_y(k, BB - 1)
                else:
                    softmax_sum(k.slab + (NC - 1))
                chain = router(k)
                next(chain)
                ahead(0)
                ahead(1)
                next(chain)
                if not k.last:
                    probs_lo(k.slab + (NC - 1))
                ahead(2)
                if not k.last:
                    out_lo(k.slab + (NC - 1), NC - 1, SB)
                next(chain)
                next(chain)
                dve.wait_ge(coef_spread, k.i + 1)
                for m in range(2):
                    scale(0, m)
                for m in range(2):
                    scaled_lo(0, m)
                scale(0, 2)
                scaled_lo(0, 2)
                for m in range(3, NC):
                    scale(0, m)
                    ahead(m)
                    scaled_lo(0, m)
                    if m == 3:
                        dve.wait_ge(spans_ready, k.i + 1)
                for e in range(NE):
                    if e > 0:
                        with dve.Fori(0, NC // RING) as g:
                            for s in range(RING):
                                scale(e, e * 2 * NC + s, g)
                                ahead(e * 2 * NC + s, g)
                                scaled_lo(e, s, g)

                    def shares(first, n):
                        end = k.last and e == NE - 1
                        with dve.Fori(0, NC // RING - end) as g:
                            for s in range(RING):
                                share(e, (e * 2 + 1) * NC + s, g, (first, n))
                        if end:
                            for m in range(NC - RING, NC):
                                share(e, (e * 2 + 1) * NC + m, 0, (first, n), m < NC - 3)

                    for_span(dve, k, e, shares)

            def iteration(i, last):
                k = Counts(dve, i, last)

                def ahead(off):
                    lo_piece(k.pos + (off + 3), (off + 3) % RING)

                if last:
                    turned_y(k, 0)
                    for b in range(FIRST, BB):
                        for c in range(NC):
                            ahead((b - FIRST) * NC + c)
                            if c == 4:
                                turned_y(k, b - 1)
                    experts(k)
                    return
                mixed_lo(i + 1, range(4))
                turned_y(k, 0)
                mixed_lo(i + 1, (4, 5))
                turned_y(k, 1)
                mixed_lo(i + 1, (6, 7))
                for m in range(NC):
                    slab = k.slab + m
                    if m >= NWOVEN:
                        off = slab_pos(m)
                        softmax_sum(slab - 1)
                        rotate(0, k.pos + (off + 1))
                        rotated_lo(slab, 0, k.use[0] + (2 * m + 2))
                        rotate(1, k.pos + (off + 2))
                        rotated_lo(slab, 1, k.use[1] + (m + 2))
                        probs_lo(slab - 1)
                        ahead(off)
                        out_lo(slab - 1, m - 1, out_banks(m))
                        if m == NWOVEN:
                            turned_y(k, BB - 1)
                        ahead(off + 1)
                        values_lo(slab)
                        ahead(off + 2)
                        softmax_max(slab)
                        continue
                    for w, piece in enumerate(order(m)):
                        off = slab_pos(m) + w
                        ahead(off)
                        if piece == "q":
                            if m > 0:
                                softmax_sum(slab - 1)
                            rotate(0, k.pos + (off + 1))
                            rotated_lo(slab, 0, k.use[0] + (2 * m + 2))
                        elif piece == "k":
                            rotate(1, k.pos + (off + 1))
                            rotated_lo(slab, 1, k.use[1] + (m + 2))
                            if m > 0:
                                probs_lo(slab - 1)
                        elif piece == "v":
                            if m > 0:
                                out_lo(slab - 1, m - 1, out_banks(m))
                        elif piece == 4:
                            values_lo(slab)
                        elif piece == 6 and m > 0:
                            turned_y(k, m + FIRST - 1)
                    softmax_max(slab)
                experts(k)

                def split_next(part):
                    with dve.If(i < NBLK - 2):
                        split_x(i + 2, [part])

                project(k.pos + POS_O, i + 1, k.slab, [k.use[j] + (USE_SLABS[j] + NF // 2) for j in range(2)],
                        split_next)

            with dve.Fori(0, NBLK - 1) as i:
                iteration(i, False)
            iteration(NBLK - 1, True)


def kernel(**inputs):
    import concourse.bacc as _bacc
    from concourse.bass_utils import run_bass_kernel_spmd as _run

    a = {k: np.asarray(v) for k, v in inputs.items()}

    def pieces(w):
        return np.ascontiguousarray(w.reshape(NC, P, NC, P).transpose(2, 1, 0, 3)).reshape(NC, P, D)

    def even_odd(w):
        return w.reshape(D, HEADS, DH // 2, 2).transpose(0, 1, 3, 2).reshape(D, D)

    x = a["x"].reshape(B * T, D)
    arrays = {
        "x_pairs": np.ascontiguousarray(x.reshape(NBLK, NP, P, D).transpose(0, 2, 1, 3)),
        "x_cols": np.ascontiguousarray(x.reshape(NBLK, BT, NC, P).transpose(0, 3, 2, 1)),
        "ids_mix": a["itok_B_0_15"].reshape(1, B),
        "ids_adapter": a["itok_B_1_14"].reshape(1, B),
        "mix_w": a["L0_cond_weights"],
        "wq": pieces(even_odd(a["L0_attn_Wq"])),
        "wk": pieces(even_odd(a["L0_attn_Wk"])),
        "wv": pieces(a["L0_attn_Wv"]),
        "wo": pieces(a["L0_attn_Wo"]),
        "adapter_w": np.ascontiguousarray(a["L0_cond2_weight"].transpose(0, 2, 1)).reshape(-1, P, D),
        "gate_w": np.ascontiguousarray(a["L0_ffn_gate_w"][:D].reshape(NC, P, NE).transpose(1, 0, 2)),
        "gate_last": a["L0_ffn_gate_w"][D:D + 1],
        "gate_b": a["L0_ffn_gate_b"].reshape(1, NE),
        "w1": np.concatenate([pieces(w) for w in a["L0_ffn_w1"]]),
        "b1": np.ascontiguousarray(a["L0_ffn_b1"].reshape(NE, NC, P).transpose(2, 0, 1)),
        "w2": np.concatenate([pieces(w) for w in a["L0_ffn_w2"]]),
        "b2": np.ascontiguousarray(a["L0_ffn_b2"].reshape(NE, NC, P).transpose(2, 0, 1)),
        "consts": shape_constants(),
    }
    nc = _bacc.Bacc("TRN2", target_bir_lowering=False, num_devices=1)
    args = [nc.dram_tensor(f"in_{n}", v.shape, mybir.dt.from_np(v.dtype), kind="ExternalInput").ap()
            for n, v in arrays.items()]
    args.append(nc.dram_tensor("out_0", (NBLK, P, NC, BT), F32, kind="ExternalOutput").ap())
    build(nc, *args)
    r = _run(nc, [{f"in_{n}": v for n, v in arrays.items()}], core_ids=[0])
    got = r.results[0]["out_0"]
    return np.ascontiguousarray(got.transpose(0, 3, 2, 1)).reshape(B, T, D)
```
